# Optimizing a Trainium2 kernel written in Bass

```python
import numpy as np
import jax
import jax.numpy as jnp

def _softmax(x, axis=-1):
    return jax.nn.softmax(x, axis=axis)

def _gelu(x):
    return jax.nn.gelu(x, approximate=True)

def _silu(x):
    return jax.nn.silu(x)

def _sigmoid(x):
    return jax.nn.sigmoid(x)

def _layernorm(x, axis=-1, eps=1e-05):
    m = jnp.mean(x, axis=axis, keepdims=True)
    v = jnp.var(x, axis=axis, keepdims=True)
    return (x - m) / jnp.sqrt(v + eps)

def _scatter_add(tgt, idx, src, axis=0):
    return tgt.at[idx].add(src)

def _segment_sum(src, seg, n):
    return jax.ops.segment_sum(src, seg, n)
kernel_name = 'mk_hybrid_d1_jaxref_r8_1b7d6d'

def setup_inputs(seed: int=0):
    np.random.seed(seed)
    _w = jnp.asarray

    def _L0_attn_a_setup():
        import jax, jax.numpy as jnp
        import numpy as np
        HIDDEN = 128
        N_HEAD = 16
        HEAD_DIM = HIDDEN // N_HEAD
        BATCH = 1
        SEQ = 512
        THETA = 10000.0

        def _rope_cos_sin(seq_len, head_dim, dtype=jnp.float32):
            inv_freq = 1.0 / THETA ** (jnp.arange(0, head_dim, 2, dtype=dtype) / head_dim)
            t = jnp.arange(seq_len, dtype=dtype)
            freqs = jnp.outer(t, inv_freq)
            return (jnp.cos(freqs), jnp.sin(freqs))

        def _apply_rope(x, cos, sin):
            x2 = x.reshape(*x.shape[:-1], -1, 2)
            x_re, x_im = (x2[..., 0], x2[..., 1])
            c = cos[None, :, None, :]
            s = sin[None, :, None, :]
            out_re = x_re * c - x_im * s
            out_im = x_re * s + x_im * c
            out = jnp.stack([out_re, out_im], axis=-1)
            return out.reshape(x.shape)
        key = jax.random.key(seed)
        kx, kq, kk, kv = jax.random.split(key, 4)
        scale = 1.0 / np.sqrt(HIDDEN)
        return {'x': jax.random.normal(kx, (BATCH, SEQ, HIDDEN), dtype=jnp.float32), 'wq': jax.random.normal(kq, (HIDDEN, HIDDEN), dtype=jnp.float32) * scale, 'wk': jax.random.normal(kk, (HIDDEN, HIDDEN), dtype=jnp.float32) * scale, 'wv': jax.random.normal(kv, (HIDDEN, HIDDEN), dtype=jnp.float32) * scale}
    _L0_attn_a_in = _L0_attn_a_setup()

    def _L0_attn_b_setup():
        import jax, jax.numpy as jnp
        import numpy as np
        D_MODEL = 128
        D_STATE = 128
        D_CONV = 4
        EXPAND = 2
        HEADDIM = 64
        CHUNK = 32
        D_INNER = EXPAND * D_MODEL
        NHEADS = D_INNER // HEADDIM
        CONV_DIM = D_INNER + 2 * D_STATE
        D_IN_PROJ = 2 * D_INNER + 2 * D_STATE + NHEADS
        EPS = 1e-05

        def rmsnorm(x, w, eps=EPS):
            return x * jax.lax.rsqrt(jnp.mean(x * x, axis=-1, keepdims=True) + eps) * w

        def _ssd(xd, a, Bm, Cm):
            b, l, h, p = xd.shape
            n = Bm.shape[-1]
            nc = l // CHUNK
            xd = xd.reshape(b, nc, CHUNK, h, p)
            a = a.reshape(b, nc, CHUNK, h).transpose(0, 3, 1, 2)
            Bm = Bm.reshape(b, nc, CHUNK, n)
            Cm = Cm.reshape(b, nc, CHUNK, n)
            a_cs = jnp.cumsum(a, axis=-1)
            diff = a_cs[..., :, None] - a_cs[..., None, :]
            mask = jnp.tril(jnp.ones((CHUNK, CHUNK), bool))
            Lm = jnp.exp(jnp.where(mask, diff, 0.0)) * mask
            Y_diag = jnp.einsum('bcln,bcsn,bhcls,bcshp->bclhp', Cm, Bm, Lm, xd)
            decay_states = jnp.exp(a_cs[..., -1:] - a_cs)
            states = jnp.einsum('bcln,bhcl,bclhp->bchpn', Bm, decay_states, xd)
            tot = jnp.pad(a_cs[..., -1], ((0, 0), (0, 0), (1, 0)))
            tot_cs = jnp.cumsum(tot, axis=-1)
            dchunk = tot_cs[..., :, None] - tot_cs[..., None, :]
            cmask = jnp.tril(jnp.ones((nc + 1, nc + 1), bool))
            dchunk = jnp.exp(jnp.where(cmask, dchunk, 0.0)) * cmask
            states = jnp.concatenate([jnp.zeros_like(states[:, :1]), states], axis=1)
            new_states = jnp.einsum('bhzc,bchpn->bzhpn', dchunk, states)
            init_states = new_states[:, :-1]
            Y_off = jnp.einsum('bcln,bchpn,bhcl->bclhp', Cm, init_states, jnp.exp(a_cs))
            return (Y_diag + Y_off).reshape(b, l, h, p)
        key = jax.random.key(seed)
        ks = jax.random.split(key, 8)
        B, L = (2, 256)

        def w(k, shape, sc=0.02):
            return jax.random.normal(k, shape, jnp.float32) * sc
        return {'x': jax.random.normal(ks[0], (B, L, D_MODEL), jnp.float32), 'norm_w': jnp.ones((D_MODEL,), jnp.float32), 'in_proj_w': w(ks[1], (D_IN_PROJ, D_MODEL)), 'conv_w': w(ks[2], (CONV_DIM, 1, D_CONV), 0.2), 'conv_b': jnp.zeros((CONV_DIM,), jnp.float32), 'dt_bias': w(ks[3], (NHEADS,), 1.0), 'A_log': jnp.log(1.0 + 15.0 * jax.random.uniform(ks[4], (NHEADS,), jnp.float32)), 'D': jnp.ones((NHEADS,), jnp.float32), 'gnorm_w': jnp.ones((D_INNER,), jnp.float32), 'out_proj_w': w(ks[5], (D_MODEL, D_INNER))}
    _L0_attn_b_in = _L0_attn_b_setup()

    def _L0_ffn_setup():
        import math
        import jax, jax.numpy as jnp
        import numpy as np
        D_MODEL = 128
        D_FF = 512
        N_EXPERTS = 8
        CAPACITY_FACTOR = 1.25
        L, B = (64, 8)

        def _route(tokens, router_w):
            T = tokens.shape[0]
            E = router_w.shape[0]
            capacity = int(math.ceil(T / E * CAPACITY_FACTOR))
            logits = tokens @ router_w.T
            probs = jax.nn.softmax(logits, axis=-1)
            top1_idx = jnp.argmax(probs, axis=-1)
            top1_prob = jnp.max(probs, axis=-1)
            order = jnp.lexsort((-top1_prob, top1_idx))
            sorted_e = top1_idx[order]
            counts = jnp.bincount(top1_idx, length=E)
            start = jnp.cumsum(counts) - counts
            pos_in_group = jnp.arange(T) - start[sorted_e]
            keep_sorted = pos_in_group < capacity
            keep = jnp.zeros((T,), bool).at[order].set(keep_sorted)
            return jnp.where(keep, top1_idx, 0).astype(jnp.int32)
        key = jax.random.key(seed)
        ks = jax.random.split(key, 6)
        s_in = 1.0 / math.sqrt(D_MODEL)
        s_ff = 1.0 / math.sqrt(D_FF)
        return {'x': jax.random.normal(ks[0], (L, B, D_MODEL), dtype=jnp.float32), 'router_w': jax.random.uniform(ks[1], (N_EXPERTS, D_MODEL), minval=-s_in, maxval=s_in), 'W1': jax.random.uniform(ks[2], (N_EXPERTS, D_MODEL, D_FF), minval=-s_in, maxval=s_in), 'b1': jax.random.uniform(ks[3], (N_EXPERTS, D_FF), minval=-s_in, maxval=s_in), 'W2': jax.random.uniform(ks[4], (N_EXPERTS, D_FF, D_MODEL), minval=-s_ff, maxval=s_ff), 'b2': jax.random.uniform(ks[5], (N_EXPERTS, D_MODEL), minval=-s_ff, maxval=s_ff)}
    _L0_ffn_in = _L0_ffn_setup()
    _d = {'L0_attn_a_x': _L0_attn_a_in['x'], 'L0_attn_a_wq': _L0_attn_a_in['wq'], 'L0_attn_a_wk': _L0_attn_a_in['wk'], 'L0_attn_a_wv': _L0_attn_a_in['wv'], 'L0_attn_b_norm_w': _L0_attn_b_in['norm_w'], 'L0_attn_b_in_proj_w': _L0_attn_b_in['in_proj_w'], 'L0_attn_b_conv_w': _L0_attn_b_in['conv_w'], 'L0_attn_b_conv_b': _L0_attn_b_in['conv_b'], 'L0_attn_b_dt_bias': _L0_attn_b_in['dt_bias'], 'L0_attn_b_A_log': _L0_attn_b_in['A_log'], 'L0_attn_b_D': _L0_attn_b_in['D'], 'L0_attn_b_gnorm_w': _L0_attn_b_in['gnorm_w'], 'L0_attn_b_out_proj_w': _L0_attn_b_in['out_proj_w'], 'L0_ffn_router_w': _L0_ffn_in['router_w'], 'L0_ffn_W1': _L0_ffn_in['W1'], 'L0_ffn_b1': _L0_ffn_in['b1'], 'L0_ffn_W2': _L0_ffn_in['W2'], 'L0_ffn_b2': _L0_ffn_in['b2']}
    _x0 = _d['L0_attn_a_x']
    _d['L0_attn_a_x'] = jax.random.normal(jax.random.fold_in(jax.random.key(seed), 1), (2, 1024, 128), dtype=_x0.dtype)
    del _x0
    return _d

def reference(L0_attn_a_x, L0_attn_a_wq, L0_attn_a_wk, L0_attn_a_wv, L0_attn_b_norm_w, L0_attn_b_in_proj_w, L0_attn_b_conv_w, L0_attn_b_conv_b, L0_attn_b_dt_bias, L0_attn_b_A_log, L0_attn_b_D, L0_attn_b_gnorm_w, L0_attn_b_out_proj_w, L0_ffn_router_w, L0_ffn_W1, L0_ffn_b1, L0_ffn_W2, L0_ffn_b2):

    def _L0_attn_a_ref(x, wq, wk, wv):
        import jax, jax.numpy as jnp
        import numpy as np
        HIDDEN = 128
        N_HEAD = 16
        HEAD_DIM = HIDDEN // N_HEAD
        BATCH = 1
        SEQ = 512
        THETA = 10000.0

        def _rope_cos_sin(seq_len, head_dim, dtype=jnp.float32):
            inv_freq = 1.0 / THETA ** (jnp.arange(0, head_dim, 2, dtype=dtype) / head_dim)
            t = jnp.arange(seq_len, dtype=dtype)
            freqs = jnp.outer(t, inv_freq)
            return (jnp.cos(freqs), jnp.sin(freqs))

        def _apply_rope(x, cos, sin):
            x2 = x.reshape(*x.shape[:-1], -1, 2)
            x_re, x_im = (x2[..., 0], x2[..., 1])
            c = cos[None, :, None, :]
            s = sin[None, :, None, :]
            out_re = x_re * c - x_im * s
            out_im = x_re * s + x_im * c
            out = jnp.stack([out_re, out_im], axis=-1)
            return out.reshape(x.shape)
        B, S, _ = x.shape
        xq = (x @ wq.T).reshape(B, S, N_HEAD, HEAD_DIM).astype(jnp.float32)
        xk = (x @ wk.T).reshape(B, S, N_HEAD, HEAD_DIM).astype(jnp.float32)
        xv = (x @ wv.T).reshape(B, S, N_HEAD, HEAD_DIM).astype(jnp.float32)
        cos, sin = _rope_cos_sin(S, HEAD_DIM)
        q = _apply_rope(xq, cos, sin)
        k = _apply_rope(xk, cos, sin)
        scores = jnp.einsum('bqhd,bkhd->bhqk', q, k) / jnp.sqrt(jnp.asarray(HEAD_DIM, dtype=q.dtype))
        attn = jax.nn.softmax(scores, axis=-1)
        out = jnp.einsum('bhqk,bkhd->bqhd', attn, xv)
        return out.reshape(B, S, N_HEAD * HEAD_DIM)

    def _L0_attn_b_ref(x, norm_w, in_proj_w, conv_w, conv_b, dt_bias, A_log, D, gnorm_w, out_proj_w):
        import jax, jax.numpy as jnp
        import numpy as np
        D_MODEL = 128
        D_STATE = 128
        D_CONV = 4
        EXPAND = 2
        HEADDIM = 64
        CHUNK = 32
        D_INNER = EXPAND * D_MODEL
        NHEADS = D_INNER // HEADDIM
        CONV_DIM = D_INNER + 2 * D_STATE
        D_IN_PROJ = 2 * D_INNER + 2 * D_STATE + NHEADS
        EPS = 1e-05

        def rmsnorm(x, w, eps=EPS):
            return x * jax.lax.rsqrt(jnp.mean(x * x, axis=-1, keepdims=True) + eps) * w

        def _ssd(xd, a, Bm, Cm):
            b, l, h, p = xd.shape
            n = Bm.shape[-1]
            nc = l // CHUNK
            xd = xd.reshape(b, nc, CHUNK, h, p)
            a = a.reshape(b, nc, CHUNK, h).transpose(0, 3, 1, 2)
            Bm = Bm.reshape(b, nc, CHUNK, n)
            Cm = Cm.reshape(b, nc, CHUNK, n)
            a_cs = jnp.cumsum(a, axis=-1)
            diff = a_cs[..., :, None] - a_cs[..., None, :]
            mask = jnp.tril(jnp.ones((CHUNK, CHUNK), bool))
            Lm = jnp.exp(jnp.where(mask, diff, 0.0)) * mask
            Y_diag = jnp.einsum('bcln,bcsn,bhcls,bcshp->bclhp', Cm, Bm, Lm, xd)
            decay_states = jnp.exp(a_cs[..., -1:] - a_cs)
            states = jnp.einsum('bcln,bhcl,bclhp->bchpn', Bm, decay_states, xd)
            tot = jnp.pad(a_cs[..., -1], ((0, 0), (0, 0), (1, 0)))
            tot_cs = jnp.cumsum(tot, axis=-1)
            dchunk = tot_cs[..., :, None] - tot_cs[..., None, :]
            cmask = jnp.tril(jnp.ones((nc + 1, nc + 1), bool))
            dchunk = jnp.exp(jnp.where(cmask, dchunk, 0.0)) * cmask
            states = jnp.concatenate([jnp.zeros_like(states[:, :1]), states], axis=1)
            new_states = jnp.einsum('bhzc,bchpn->bzhpn', dchunk, states)
            init_states = new_states[:, :-1]
            Y_off = jnp.einsum('bcln,bchpn,bhcl->bclhp', Cm, init_states, jnp.exp(a_cs))
            return (Y_diag + Y_off).reshape(b, l, h, p)
        res = x
        u = rmsnorm(x, norm_w)
        zxbcdt = u @ in_proj_w.T
        z, xBC, dt = jnp.split(zxbcdt, [D_INNER, D_INNER + CONV_DIM], axis=-1)
        xBC_t = jnp.pad(xBC.transpose(0, 2, 1), ((0, 0), (0, 0), (D_CONV - 1, 0)))
        conv = jax.lax.conv_general_dilated(xBC_t, conv_w, (1,), 'VALID', dimension_numbers=('NCH', 'OIH', 'NCH'), feature_group_count=CONV_DIM)
        xBC = jax.nn.silu(conv.transpose(0, 2, 1) + conv_b)
        xs, Bm, Cm = jnp.split(xBC, [D_INNER, D_INNER + D_STATE], axis=-1)
        dt = jax.nn.softplus(dt + dt_bias)
        A = -jnp.exp(A_log)
        xh = xs.reshape(xs.shape[0], xs.shape[1], NHEADS, HEADDIM)
        y = _ssd(xh * dt[..., None], dt * A, Bm, Cm)
        y = y + D[None, None, :, None] * xh
        y = y.reshape(xs.shape)
        y = rmsnorm(y * jax.nn.silu(z), gnorm_w)
        return res + y @ out_proj_w.T

    def _L0_ffn_ref(x, router_w, W1, b1, W2, b2):
        import math
        import jax, jax.numpy as jnp
        import numpy as np
        D_MODEL = 128
        D_FF = 512
        N_EXPERTS = 8
        CAPACITY_FACTOR = 1.25
        L, B = (64, 8)

        def _route(tokens, router_w):
            T = tokens.shape[0]
            E = router_w.shape[0]
            capacity = int(math.ceil(T / E * CAPACITY_FACTOR))
            logits = tokens @ router_w.T
            probs = jax.nn.softmax(logits, axis=-1)
            top1_idx = jnp.argmax(probs, axis=-1)
            top1_prob = jnp.max(probs, axis=-1)
            order = jnp.lexsort((-top1_prob, top1_idx))
            sorted_e = top1_idx[order]
            counts = jnp.bincount(top1_idx, length=E)
            start = jnp.cumsum(counts) - counts
            pos_in_group = jnp.arange(T) - start[sorted_e]
            keep_sorted = pos_in_group < capacity
            keep = jnp.zeros((T,), bool).at[order].set(keep_sorted)
            return jnp.where(keep, top1_idx, 0).astype(jnp.int32)
        Lx, Bx, D = x.shape
        T = Lx * Bx
        E = router_w.shape[0]
        tokens = x.reshape(T, D)
        final_e = _route(tokens, router_w)
        out = jnp.zeros_like(tokens)
        for e in range(E):
            h = jax.nn.relu(tokens @ W1[e] + b1[e])
            y = h @ W2[e] + b2[e]
            out = out + jnp.where((final_e == e)[:, None], y, 0.0)
        return out.reshape(Lx, Bx, D)
    x = L0_attn_a_x
    x = x + _L0_attn_a_ref(_layernorm(x, axis=-1), L0_attn_a_wq, L0_attn_a_wk, L0_attn_a_wv)
    x = x + _L0_ffn_ref(_layernorm(x, axis=-1), L0_ffn_router_w, L0_ffn_W1, L0_ffn_b1, L0_ffn_W2, L0_ffn_b2)
    x = x + _L0_attn_b_ref(_layernorm(x, axis=-1), L0_attn_b_norm_w, L0_attn_b_in_proj_w, L0_attn_b_conv_w, L0_attn_b_conv_b, L0_attn_b_dt_bias, L0_attn_b_A_log, L0_attn_b_D, L0_attn_b_gnorm_w, L0_attn_b_out_proj_w)
    x = x + _L0_ffn_ref(_layernorm(x, axis=-1), L0_ffn_router_w, L0_ffn_W1, L0_ffn_b1, L0_ffn_W2, L0_ffn_b2)
    return x

_drawn_inputs = setup_inputs


def setup_inputs(seed=0):
    import zlib

    import numpy as np

    out = dict(_drawn_inputs(seed))
    spreads = {'L0_attn_b_norm_w': (1.0, 0.2),
     'L0_attn_b_conv_b': (0.0, 0.1),
     'L0_attn_b_D': (1.0, 0.2),
     'L0_attn_b_gnorm_w': (1.0, 0.2)}
    factors = {'L0_attn_b_dt_bias': 6.076, 'L0_attn_b_A_log': 8.0}
    for name, (base, spread) in spreads.items():
        noise = np.random.default_rng([zlib.crc32(name.encode()), seed]).standard_normal(out[name].shape)
        drawn = base * np.exp(spread * noise) if base else spread * noise
        out[name] = jnp.asarray(drawn.astype(out[name].dtype))
    for name, factor in factors.items():
        out[name] = (out[name] * factor).astype(out[name].dtype)
    return out
```

```python
from contextlib import ExitStack

import concourse.bass as bass
from concourse import mybir

F32 = mybir.dt.float32
BF16 = mybir.dt.bfloat16
U32 = mybir.dt.uint32
ALU = mybir.AluOpType
ACT = mybir.ActivationFunctionType
AX = mybir.AxisListType

P = 128
BATCH, SEQ, D = 2, 1024, 128
TOK = BATCH * SEQ
TILES = TOK // P
BT = SEQ // P
HEADS, HD = 16, 8
UNITS = BATCH * HEADS
EPS = 1e-5
EXPERTS, FF = 8, 512
FT = FF // P
CAP = 320
CT = 3
SLOTS = (EXPERTS - 1) * CAP
ROWS = SLOTS + TOK
ROW = D + 1
FILL = 112
QUAD = 32
EARLY = 6
STEPS = 4 * TILES
RANK_RING = 6
INNER, STATE, TAPS = 256, 128, 4
SHEADS, SW = 4, 64
XC = INNER // P
CONV = XC + 2
PROJ = 2 * INNER + 2 * STATE + SHEADS
LAST = P - 1
TINY = 1e-9
PARTS = 3
SROWS = PARTS * PARTS * HD
KROWS = 96
ATT_SCALE = float(HD) ** -0.5
FINISH = 6
ROWS_OUT = 9
RING = 4
LOADS = PARTS + 1
HALF = 512
VCOL = 32


def bass_hybrid(nc, t, out, stage=9):
    ctx = ExitStack()
    with ctx:
        def sb(name, shape, dt=F32):
            return ctx.enter_context(nc.sbuf_tensor(name, shape, dt))

        def pb(name, shape, dt=F32):
            return ctx.enter_context(nc.psum_tensor(name, shape, dt))

        def sem(name):
            return ctx.enter_context(nc.semaphore(name))

        def dram(name, shape, dt=F32):
            return nc.dram_tensor(name, shape, dt, kind="Internal").ap()

        qparts_dram = dram("qparts_dram", [UNITS, PARTS, HD, SEQ], BF16)
        kparts_dram = dram("kparts_dram", [UNITS, PARTS, HD, SEQ], BF16)

        sorted_dram = [dram(f"sorted_dram{f}", [ROWS, ROW]) for f in range(2)]
        y_dram = [dram(f"y_dram{f}", [TOK + SLOTS, D]) for f in range(2)]

        x = sb("x", [P, TILES, D])
        xn = sb("xn", [P, TILES, ROW])
        xnT = sb("xnT", [P, TOK])
        stats = sb("stats", [P, TILES, 6])
        meanvar = sb("meanvar", [P, TILES, 2])
        rstd = sb("rstd", [P, TILES])
        neghalf = sb("neghalf", [P, TILES])
        ident = sb("ident", [P, P])
        ident16 = sb("ident16", [P, P], BF16)

        w1 = sb("w1", [P, EXPERTS, FF])
        w2 = sb("w2", [P, EXPERTS, FT, D])
        b1T = sb("b1T", [P, EXPERTS * FT])
        b1rows = sb("b1rows", [EXPERTS * FT, P])
        b2 = sb("b2", [P, EXPERTS, D])
        router = sb("router", [EXPERTS, D])
        routerT = sb("routerT", [P, QUAD])
        left = sb("left", [P, EXPERTS])
        own_row = sb("own_row", [P, TILES])
        tri_tiny = sb("tri_tiny", [P, 7 * P])
        ones = sb("ones", [P, P])
        zeros = sb("zeros", [P, D])
        z_log = sb("z_log", [P, TILES, EXPERTS])
        e_log = sb("e_log", [P, TILES, EXPERTS])
        w_log = sb("w_log", [P, TILES, EXPERTS])
        onehot = sb("onehot", [P, TILES, EXPERTS], BF16)
        r8 = sb("r8", [P, 9, TILES])
        slot = sb("slot", [P, TILES], U32)

        win_rows = sb("win_rows", [P, 6, P])
        wdt_rows = sb("wdt_rows", [SHEADS, P])
        wout_rows = sb("wout_rows", [P, INNER])
        winT = sb("winT", [P, 6 * P + SHEADS])
        woutT = sb("woutT", [P, XC, D])
        norm_w = sb("norm_w", [P, 1])
        gnorm_w = sb("gnorm_w", [P, XC])
        conv_w = sb("conv_w", [P, CONV, TAPS])
        conv_b = sb("conv_b", [P, CONV])
        d_col = sb("d_col", [P, XC])
        dt_bias = sb("dt_bias", [P, SHEADS])
        a_log = sb("a_log", [P, SHEADS])
        neg_a = sb("neg_a", [P, SHEADS])
        after = sb("after", [P, P])
        upto = sb("upto", [P, P])
        dt = sb("dt", [P, TILES, SHEADS])
        log_decay = sb("log_decay", [P, TILES, SHEADS])
        sp_tmp = sb("sp_tmp", [P, 6, TILES * SHEADS])
        rms = sb("rms", [P, TILES])
        ysum = sb("ysum", [P, TILES])

        scope = ExitStack()

        def sb(name, shape, dt=F32):
            return scope.enter_context(nc.sbuf_tensor(name, shape, dt))

        rot = sb("rot", [P, P])
        cosT = sb("cosT", [P, SEQ])
        sinT = sb("sinT", [P, SEQ])
        wqkv = sb("wqkv", [P, 3, P])
        wT = sb("wT", [P, 5, P])
        rope_a = sb("rope_a", [P, RING, HALF])
        rope_b = sb("rope_b", [P, RING, HALF])
        parts16 = sb("parts16", [P, 2, PARTS, TOK], BF16)
        values = sb("values", [P, UNITS, BT, HD])
        vstage = sb("vstage", [P, 2, BT, VCOL])
        qa = sb("qa", [P, 4, SEQ], BF16)
        ka = sb("ka", [P, 4, SEQ], BF16)
        negmax = sb("negmax", [P, 2, BT])
        maxrest = sb("maxrest", [P, 2, BT])
        maxparts = sb("maxparts", [P, PARTS, BT], BF16)
        maxrows = sb("maxrows", [PARTS * BT, 2, P], BF16)
        probs = sb("probs", [P, 4, SEQ])
        o_sb = sb("o_sb", [P, HALF])
        osum = sb("osum", [P, BT, HD + 1])
        orec = sb("orec", [P, BT])
        att = sb("att", [P, UNITS, BT, HD])


        scope.close()
        diag = sb("diag", [P, TILES, P])
        prow = sb("prow", [P, TOK])
        before = sb("before", [P, RANK_RING, HALF], BF16)
        hidden = sb("hidden", [P, 2, FT, HALF])
        y_sb = sb("y_sb", [P, 2, 4, D])
        sorted_x = sb("sorted_x", [P, EXPERTS, CT, ROW])
        dest = sb("dest", [P, EXPERTS, CT], U32)
        sortedT = sb("sortedT", [P, SLOTS])
        gathered = sb("gathered", [P, TILES, D])
        scope.close()
        before_conv = sb("before_conv", [P, CONV, BATCH, TAPS - 1 + SEQ])
        conv_acc = sb("conv_acc", [P, 2, SEQ])
        un = conv_acc[:].rearrange("p a n -> p (a n)").rearrange("p (t d) -> p t d", t=TILES)
        xbc = sb("xbc", [P, CONV, TOK])
        gate = sb("gate", [P, XC, TOK])
        seg = sb("seg", [P, 2, SHEADS, P])
        decay = sb("decay", [P, 2, SHEADS, P])
        from_start = sb("from_start", [P, 2, SHEADS, P])
        b_tok = sb("b_tok", [P, 2, STATE])
        cb = sb("cb", [P, 2, P])
        mix = sb("mix", [P, 2, SHEADS, P])
        c_dec = sb("c_dec", [P, 2, SHEADS, P])
        xd = sb("xd", [P, 2, SHEADS, SW])
        xdd = sb("xdd", [P, 2, SHEADS, SW])
        state = sb("state", [P, BATCH, 2, SHEADS, SW])
        st_tmp = sb("st_tmp", [P, SHEADS, SW])
        y_dx = sb("y_dx", [P, XC, P])
        yg = sb("yg", [P, 2, XC, P])
        ysq = sb("ysq", [P, 2, XC, P])
        scope.close()

        mbank = pb("mbank", [P, 2, SEQ])
        ebank = pb("ebank", [P, 2, HALF])
        obank = pb("obank", [P, HALF])
        tbank = pb("tbank", [P, HALF])
        mtrans = tbank[:].bitcast(BF16)[0:PARTS * BT, 0:P]
        bank = [mbank[:, 0, 0:HALF], mbank[:, 0, HALF:SEQ], mbank[:, 1, 0:HALF], mbank[:, 1, HALF:SEQ],
                ebank[:, 0, :], ebank[:, 1, :], obank[:], tbank[:]]

        s_const = sem("s_const")
        s_w = sem("s_w")
        s_x = sem("s_x")
        s_xin = [sem(f"s_xin{b}") for b in range(BATCH)]
        s_init = sem("s_init")
        s_id16 = sem("s_id16")
        s_dve = sem("s_dve")
        s_ln = sem("s_ln")
        s_rstd = sem("s_rstd")
        s_pool = sem("s_pool")
        s_xn = sem("s_xn")
        s_tr = sem("s_tr")
        s_trc = sem("s_trc")
        s_wt = sem("s_wt")
        s_wtc = sem("s_wtc")
        s_proj = sem("s_proj")
        s_projc = sem("s_projc")
        s_val = sem("s_val")
        s_valc = sem("s_valc")
        s_rs = sem("s_rs")
        s_p1 = sem("s_p1")
        s_r1 = sem("s_r1")
        s_p2 = sem("s_p2")
        s_r2 = sem("s_r2")
        s_parts = sem("s_parts")
        s_pl = sem("s_pl")
        s_pstore = [sem(f"s_pstore{b}") for b in range(BATCH)]
        s_load = [sem(f"s_load{i}") for i in range(4)]
        s_vst = sem("s_vst")
        s_ms = sem("s_ms")
        s_mx = sem("s_mx")
        s_mp = sem("s_mp")
        s_mt = sem("s_mt")
        s_mc = sem("s_mc")
        s_mrow = sem("s_mrow")
        s_sc = sem("s_sc")
        s_pr = sem("s_pr")
        s_pv = sem("s_pv")
        s_oc = sem("s_oc")
        s_ot = sem("s_ot")
        s_od = sem("s_od")
        s_at = sem("s_at")
        s_oa = sem("s_oa")
        s_zero = sem("s_zero")
        s_moew = sem("s_moew")
        s_ew = sem("s_ew")
        s_rt = sem("s_rt")
        s_zl = sem("s_zl")
        s_el = sem("s_el")
        s_oh = sem("s_oh")
        s_dg = sem("s_dg")
        s_pw = sem("s_pw")
        s_pwc = sem("s_pwc")
        s_bf = sem("s_bf")
        s_lt = sem("s_lt")
        s_lc = sem("s_lc")
        s_rk = sem("s_rk")
        s_slot = sem("s_slot")
        s_scat = sem("s_scat")
        s_srt = [sem(f"s_srt{i}") for i in range(EXPERTS)]
        s_dest = sem("s_dest")
        s_st = sem("s_st")
        s_stc = sem("s_stc")
        s_h = sem("s_h")
        s_ha = sem("s_ha")
        s_hv = sem("s_hv")
        s_y = sem("s_y")
        s_yc = sem("s_yc")
        s_yst = [sem(f"s_yst{i}") for i in range(2)]
        s_ysc = [sem(f"s_ysc{i}") for i in range(2)]
        s_ga = [sem(f"s_ga{i}") for i in range(4)]
        s_out = sem("s_out")
        m_w = sem("m_w")
        s_nega = sem("s_nega")
        m_wt = sem("m_wt")
        m_wc = sem("m_wc")
        m_pad = sem("m_pad")
        m_zx = sem("m_zx")
        m_zc = sem("m_zc")
        m_conv = sem("m_conv")
        m_xbc = sem("m_xbc")
        m_dt = sem("m_dt")
        m_de = sem("m_de")
        m_dec = sem("m_dec")
        m_ua = sem("m_ua")
        m_tp = sem("m_tp")
        m_g = sem("m_g")
        m_df = sem("m_df")
        m_bc = sem("m_bc")
        m_L = sem("m_L")
        m_E = sem("m_E")
        m_B = sem("m_B")
        m_gm = sem("m_gm")
        m_M = sem("m_M")
        m_CE = sem("m_CE")
        m_xd = sem("m_xd")
        m_xdd = sem("m_xdd")
        m_y = sem("m_y")
        m_s = sem("m_s")
        m_st = sem("m_st")
        m_yg = sem("m_yg")
        m_sq = sem("m_sq")
        m_o = sem("m_o")
        m_ms = sem("m_ms")
        m_rs = sem("m_rs")
        m_fin = sem("m_fin")
        m_u = sem("m_u")

        x_view = t["L0_attn_a_x"].rearrange("b (t p) d -> p (b t) d", p=P)

        def past(eng, semaphore, value):
            if not isinstance(value, int) or value > 0:
                eng.wait_ge(semaphore, value)

        def groups(eng, body):
            body(0, 0)
            with eng.Fori(1, UNITS // 4 - 1) as g:
                body(g, 1)
            body(UNITS // 4 - 1, 2)

        def hs(f, e, i):
            return (4 * FT + (EXPERTS - 1) * FT) * f + (i if e == 0 else 4 * FT + (e - 1) * FT + i)

        def conv_ready(n):
            c, b = n % CONV, n // CONV
            return 6 * (2 * b + 1) + c + 1

        def chunk_tile(i):
            return (i % 2) * BT + i // 2

        def tr_bank(k, i):
            return bank[(0 if k == 1 else 6) + i % 2]

        def acts(f):
            return (4 * FT + (EXPERTS - 1) * FT // 2) * f

        def part(n, k):
            b, side, h = (n - 1) // 4, (n - 1) // 2 % 2, (n - 1) % 2
            return parts16[:, side, k, b * SEQ + h * HALF:b * SEQ + (h + 1) * HALF]

        def ys(f, i):
            return (EXPERTS + 3) * f + i

        after_store, stored, dense_stored = [], [], []
        dense_total, sparse_total = [0, 0], [0, 0]
        for f in range(2):
            for i in range(EXPERTS + 3):
                r = ys(f, i) % 2
                if i < 4:
                    dense_total[r] += 16
                    after_store.append((s_yst[r], dense_total[r]))
                else:
                    sparse_total[r] += 16 * CT
                    after_store.append((s_ysc[r], sparse_total[r]))
                if i == 3:
                    dense_stored.append(list(dense_total))
            stored.append(list(sparse_total))

        block = ctx.enter_context(nc.Block())

        @block.sync
        def _(sp):
            sp.dma_start(x[:, 0:BT, :], x_view[:, 0:BT, :]).then_inc(s_xin[0], 16)
            for i, n in enumerate(("wq", "wk", "wv")):
                sp.dma_start(wqkv[:, i, :], t["L0_attn_a_" + n]).then_inc(s_w, 16)
            sp.dma_start(ident[:], t["ident"]).then_inc(s_w, 16)
            sp.dma_start(rot[:], t["rot"]).then_inc(s_w, 16)
            sp.dma_start(cosT[:], t["cos"]).then_inc(s_const, 16)
            sp.dma_start(sinT[:], t["sin"]).then_inc(s_const, 16)
            sp.dma_start(x[:, BT:TILES, :], x_view[:, BT:TILES, :]).then_inc(s_xin[1], 16)

            def later_loads():
                sp.dma_start(router[:], t["L0_ffn_router_w"]).then_inc(s_moew, 16)
                sp.dma_start(b1rows[:], t["L0_ffn_b1"].rearrange("e (f p) -> (e f) p", p=P)).then_inc(s_moew, 16)
                sp.dma_start(b2[:].rearrange("p e d -> p (e d)"),
                             t["L0_ffn_b2"].rearrange("e d -> (e d)").partition_broadcast(P)).then_inc(s_moew, 16)
                sp.dma_start(left[:], t["left"]).then_inc(s_moew, 16)
                sp.dma_start(own_row[:], t["own_row"]).then_inc(s_moew, 16)
                sp.dma_start(tri_tiny[:], t["tri_tiny"]).then_inc(s_moew, 16)
                sp.wait_ge(s_pool, 3)
                for f in range(2):
                    sp.dma_start(sorted_dram[f][0:SLOTS, 0:D].rearrange("(p m) d -> p m d", p=FILL),
                                 zeros[0:FILL].unsqueeze(1).to_broadcast([FILL, SLOTS // FILL, D])).then_inc(s_zero, 16)
                    sp.dma_start(sorted_dram[f][0:SLOTS, D:ROW], t["spare_row"], allow_slow_non_contiguous=True).then_inc(s_zero, 16)
                sp.dma_start(win_rows[:], t["L0_attn_b_in_proj_w"][0:6 * P, :].rearrange("(c p) d -> p c d", p=P)).then_inc(m_w, 16)
                sp.dma_start(wdt_rows[:], t["L0_attn_b_in_proj_w"][6 * P:PROJ, :]).then_inc(m_w, 16)
                sp.dma_start(wout_rows[:], t["L0_attn_b_out_proj_w"]).then_inc(m_w, 16)
                sp.dma_start(norm_w[:], t["L0_attn_b_norm_w"].unsqueeze(1)).then_inc(m_w, 16)
                sp.dma_start(gnorm_w[:], t["L0_attn_b_gnorm_w"].rearrange("(c p) -> p c", p=P),
                          allow_slow_non_contiguous=True).then_inc(m_w, 16)
                sp.dma_start(conv_w[:], t["L0_attn_b_conv_w"].rearrange("(c p) o k -> p c (o k)", p=P)).then_inc(m_w, 16)
                sp.dma_start(conv_b[:], t["L0_attn_b_conv_b"].rearrange("(c p) -> p c", p=P),
                          allow_slow_non_contiguous=True).then_inc(m_w, 16)
                for h in range(SHEADS):
                        sp.dma_start(d_col[(h % 2) * SW:(h % 2 + 1) * SW, h // 2:h // 2 + 1],
                                  t["L0_attn_b_D"][h:h + 1].partition_broadcast(SW)).then_inc(m_w, 16)
                sp.dma_start(dt_bias[:], t["L0_attn_b_dt_bias"].partition_broadcast(P)).then_inc(m_w, 16)
                sp.dma_start(a_log[:], t["L0_attn_b_A_log"].partition_broadcast(P)).then_inc(m_w, 16)
                sp.dma_start(after[:], t["after"]).then_inc(m_w, 16)
                sp.dma_start(upto[:], t["upto"]).then_inc(m_w, 16)
            def load(n, j):
                past(sp, s_sc, 16 * (n - 3))
                for a in range(PARTS):
                    src = qparts_dram[bass.ds(n, 1), a].to_broadcast([PARTS, HD, SEQ])
                    sp.dma_start(qa[a * PARTS * HD:(a + 1) * PARTS * HD, j % 4, :], src).then_inc(s_load[j % 4], 16)
                src = kparts_dram[bass.ds(n, 1)].rearrange("u c d n -> u (c d) n").to_broadcast([PARTS, PARTS * HD, SEQ])
                sp.dma_start(ka[0:SROWS, j % 4, :], src).then_inc(s_load[j % 4], 16)

            def max_rows_in(n, j):
                sp.wait_ge(s_mc, n + 1)
                for part in range(PARTS):
                    sp.dma_start(qa[KROWS + part:KROWS + part + 1, j % 4, :],
                                 maxrows[part * BT:(part + 1) * BT, j % 2, :]).then_inc(s_mrow, 16)

            for b in range(BATCH):
                for side, dst in enumerate((qparts_dram, kparts_dram)):
                    sp.wait_ge(s_parts, 2 * (2 * b + side) + 2)
                    for part in range(PARTS):
                        sp.dma_start(dst[b * HEADS:(b + 1) * HEADS, part, :, :],
                                     parts16[:, side, part, b * SEQ:(b + 1) * SEQ]).then_inc(s_pstore[b], 16)
                if b == 0:
                    sp.wait_ge(s_pstore[0], 16 * PARTS * 2)
                    sp.wait_ge(s_init, 2)
                    for n in range(3):
                        load(n, n)
            sp.wait_ge(s_pstore[1], 16 * PARTS * 2)
            max_rows_in(0, 0)

            def body(g, where):
                for j in range(4):
                    n = 4 * g + j
                    if where < 2 or j < 1:
                        load(n + 3, j + 3)
                    if where < 2 or j < 3:
                        max_rows_in(n + 1, j + 1)
                    if j == 1:
                        sp.dma_start(w1[:, bass.ds(g, 1), :], t["L0_ffn_W1"][bass.ds(g, 1)].rearrange("e d f -> d e f")).then_inc(s_ew, 16)
                    if j == 2:
                        sp.dma_start(w2[:, bass.ds(g, 1), :, :].rearrange("p e f d -> p (e f) d"),
                                     t["L0_ffn_W2"][bass.ds(g, 1)].rearrange("e (f p) d -> p (e f) d", p=P)).then_inc(s_ew, 16)
                if where == 0:
                    later_loads()

            groups(sp, body)

            def experts(f):
                for g in range(4):
                    yi = ys(f, g)
                    if g == 2:
                        sorted_rows(f)
                    sp.wait_ge(s_yc, yi + 1)
                    sp.dma_start(y_dram[f][g * HALF:(g + 1) * HALF, :].rearrange("(m p) d -> p m d", p=P),
                                 y_sb[:, yi % 2, :, :]).then_inc(s_yst[yi % 2], 16)
                for i in range(2):
                    sp.wait_ge(s_ysc[i], stored[f][i])
                for g in range(4):
                    sp.dma_start(gathered[:, 4 * g:4 * g + 4, :],
                                 y_dram[f][g * HALF:(g + 1) * HALF, :].rearrange("(m p) d -> p m d", p=P)).then_inc(s_ga[g], 16)

            def sorted_rows(f):
                sp.wait_ge(s_scat, 16 * TILES * (f + 1))
                for e in range(1, EXPERTS):
                    r0 = (e - 1) * CAP
                    sp.dma_start(sorted_x[:, e, 0:2, :], sorted_dram[f][r0:r0 + 2 * P, :].rearrange("(m p) d -> p m d", p=P)).then_inc(s_srt[e], 16)
                    sp.dma_start(sorted_x[0:CAP - 2 * P, e, 2, :], sorted_dram[f][r0 + 2 * P:r0 + CAP, :]).then_inc(s_srt[e], 16)

            if stage >= 1:
                experts(0)
            if stage >= 3:
                experts(1)
            if stage < 3:
                sp.wait_ge(s_ew, 32 * EXPERTS)
                sp.wait_ge(s_zero, 64)
                sp.wait_ge(s_moew, 16 * 6)
                sp.wait_ge(m_w, 16 * 15)
            sp.wait_ge(s_out, 16)

        @block.gpsimd
        def _(pool):
            pool.memset(zeros[:], 0.0).then_inc(s_pool, 1)
            pool.memset(neghalf[:], -0.5).then_inc(s_pool, 1)
            pool.memset(ones[:], 1.0).then_inc(s_pool, 1)
            pool.memset(routerT[:], 0.0)
            pool.memset(vstage[:], 0.0).then_inc(s_pool, 1)
            pool.wait_ge(s_pool, 4)
            pool.memset(vstage[:, :, :, HD:HD + 1], 1.0).then_inc(s_pool, 1)
            pool.memset(qa[:], 0.0).then_inc(s_init, 1)
            pool.memset(ka[:], 0.0).then_inc(s_pool, 1)
            pool.wait_ge(s_pool, 6)
            pool.memset(ka[KROWS:KROWS + PARTS, :, :], 1.0).then_inc(s_init, 1)
            pool.wait_ge(s_init, 2)
            def rsqrt(k, src, batches=range(BATCH)):
                for b in batches:
                    pool.wait_ge(s_ln, 2 * k + b + 1)
                    tl = slice(b * BT, (b + 1) * BT)
                    pool.tensor_tensor(src[:, tl], src[:, tl], neghalf[:, tl], ALU.pow).then_inc(s_rstd, 1)

            rsqrt(0, rstd)

            for n in range(1, 8 + 2):
                if n <= 8:
                    pool.wait_ge(s_projc, n)
                    pool.tensor_tensor(rope_a[:, n % RING, :], rope_a[:, n % RING, :], rope_b[:, n % RING, :], ALU.add).then_inc(s_rs, 1)
                if n >= 2:
                    pool.wait_ge(s_p1, n - 1)
                    pool.tensor_tensor(rope_b[:, (n - 1) % RING, :], rope_a[:, (n - 1) % RING, :], part(n - 1, 0),
                                       ALU.subtract).then_inc(s_r1, 1)

            pool.wait_ge(s_valc, 2 * TILES // 8)

            def max_parts(n, j):
                pool.wait_ge(s_mx, BT * (n + 1))
                past(pool, s_mt, n)
                c = 4 * n
                pool.tensor_tensor(maxparts[:, 0, :], negmax[:, j % 2, :], zeros[:, 0:BT], ALU.add).then_inc(s_pl, 1)
                pool.wait_ge(s_pl, c + 1)
                pool.tensor_tensor(maxrest[:, 0, :], negmax[:, j % 2, :], maxparts[:, 0, :], ALU.subtract).then_inc(s_pl, 1)
                pool.wait_ge(s_pl, c + 2)
                pool.tensor_tensor(maxparts[:, 1, :], maxrest[:, 0, :], zeros[:, 0:BT], ALU.add).then_inc(s_pl, 1)
                pool.wait_ge(s_pl, c + 3)
                pool.tensor_tensor(maxrest[:, 1, :], maxrest[:, 0, :], maxparts[:, 1, :], ALU.subtract).then_inc(s_pl, 1)
                pool.wait_ge(s_pl, c + 4)
                pool.tensor_tensor(maxparts[:, 2, :], maxrest[:, 1, :], zeros[:, 0:BT], ALU.add).then_inc(s_mp, 1)

            def weigh(n):
                pool.wait_ge(s_od, n + 1)
                pool.tensor_tensor(att[:, bass.ds(n, 1), :, :].rearrange("p u t d -> p (u t) d"), osum[:, :, 0:HD],
                                   orec[:].unsqueeze(2).to_broadcast([P, BT, HD]), ALU.mult).then_inc(s_at, 1)

            max_parts(0, 0)
            max_parts(1, 1)

            def body(g, where):
                for j in range(4):
                    n = 4 * g + j
                    past(pool, s_pv, 4 * (4 * g + j - 1))
                    pool.tensor_tensor(vstage[:, j % 2, :, 0:HD],
                                       values[:, bass.ds(4 * g + j, 1), :, :].rearrange("p u t d -> p (u t) d"),
                                       zeros[:, 0:BT * HD].rearrange("p (t d) -> p t d", t=BT), ALU.add).then_inc(s_vst, 1)
                    if where > 0 or j > 0:
                        weigh(n - 1)
                    if where < 2 or j < 2:
                        max_parts(n + 2, j)
                    if where == 2 and j == 2 and stage >= 1:
                        rsqrt(1, rstd, [0])

            groups(pool, body)
            weigh(UNITS - 1)

            def experts(f, k):
                rsqrt(k, rstd, [0, 1] if f else [1])
                pool.wait_ge(s_zero, 64)
                for i in range(TILES):
                    if i % 4 == 0:
                        pool.wait_ge(s_slot, 4 * f + i // 4 + 1)
                    pool.indirect_dma_start(sorted_dram[f][:, :], bass.IndirectOffsetOnAxis(ap=slot[:, i:i + 1], axis=0),
                                            xn[:, i, :], None).then_inc(s_scat, 16)
                for i in range(2):
                    pool.wait_ge(s_yst[i], dense_stored[f][i])
                for e in range(1, EXPERTS):
                    yi = ys(f, 3 + e)
                    pool.wait_ge(s_yc, yi + 1)
                    pool.wait_ge(s_dest, (EXPERTS - 1) * f + e)
                    for m in range(CT):
                        n = min(P, CAP - m * P)
                        pool.indirect_dma_start(y_dram[f][:, :], bass.IndirectOffsetOnAxis(ap=dest[0:n, e, m:m + 1], axis=0),
                                                y_sb[0:n, yi % 2, m, :], None).then_inc(s_ysc[yi % 2], 16)

            def state_space(k):
                pool.memset(before_conv[:, :, :, 0:TAPS - 1], 0.0).then_inc(m_pad, 1)
                rsqrt(k, rstd)
                rsqrt(k + 1, rms)

                def segments(i):
                    T = chunk_tile(i)
                    if i == 0:
                        pool.wait_ge(m_dec, 1)
                    past(pool, m_df, i - 1)
                    pool.tensor_tensor(seg[:, i % 2, :, :], after[:].unsqueeze(1).to_broadcast([P, SHEADS, P]),
                                       log_decay[:, T, :].unsqueeze(2).to_broadcast([P, SHEADS, P]), ALU.mult).then_inc(m_ua, 1)

                segments(0)
                for i in range(TILES + 2):
                    if i + 1 < TILES:
                        segments(i + 1)
                    if i < TILES:
                        T = chunk_tile(i)
                        pool.wait_ge(m_E, i + 1)
                        past(pool, m_y, i - 1)
                        pool.tensor_tensor(c_dec[:, i % 2, :, :], from_start[:, i % 2, :, :],
                                           xbc[:, CONV - 1, T * P:(T + 1) * P].unsqueeze(1).to_broadcast([P, SHEADS, P]),
                                           ALU.mult).then_inc(m_CE, 1)
                    if i >= 2:
                        T = chunk_tile(i - 2)
                        pool.wait_ge(m_ms, i - 1)
                        pool.tensor_tensor(ysum[:, T:T + 1], ysum[:, T:T + 1], neghalf[:, 0:1], ALU.pow).then_inc(m_rs, 1)

            if stage >= 1:
                experts(0, 1)
            if stage >= 2:
                state_space(2)
            if stage >= 3:
                experts(1, 4)

        @block.vector
        def _(dve):
            steps = [0]

            def link(ins):
                steps[0] += 1
                ins.then_inc(s_dve, 1)
                dve.wait_ge(s_dve, steps[0])

            def layernorm(b, k):
                for i in range(b * BT, (b + 1) * BT):
                    ins = dve.bn_stats(stats[:, i, :], x[:, i, :])
                link(ins)
                for i in range(b * BT, (b + 1) * BT):
                    ins = dve.bn_aggr(meanvar[:, i, :], stats[:, i, :])
                link(ins)
                tl = slice(b * BT, (b + 1) * BT)
                dve.tensor_scalar(rstd[:, tl], meanvar[:, tl, 1], EPS, None, ALU.add).then_inc(s_ln, 1)

            def normalise(b, k):
                dve.wait_ge(s_rstd, 2 * k + b + 1)
                for i in range(b * BT, (b + 1) * BT):
                    ins = dve.tensor_scalar(xn[:, i, 0:D], x[:, i, :], meanvar[:, i, 0:1], rstd[:, i:i + 1],
                                            ALU.subtract, ALU.mult)
                ins.then_inc(s_xn, 1)

            dve.wait_ge(s_w, 80)
            dve.tensor_copy(ident16[:], ident[:]).then_inc(s_id16, 1)
            for b in range(BATCH):
                dve.wait_ge(s_xin[b], 16)
                layernorm(b, 0)
            for b in range(BATCH):
                normalise(b, 0)
            def rope_products(n):
                pos = slice((n - 1) % 2 * HALF, ((n - 1) % 2 + 1) * HALF)
                dve.wait_ge(s_proj, n)
                past(dve, s_parts, n - RING)
                dve.tensor_tensor(rope_a[:, n % RING, :], bank[(2 * n) % 4], cosT[:, pos], ALU.mult)
                dve.tensor_tensor(rope_b[:, n % RING, :], bank[(2 * n + 1) % 4], sinT[:, pos], ALU.mult).then_inc(s_projc, 1)

            def second_rest(n):
                dve.wait_ge(s_p2, n)
                dve.tensor_tensor(rope_a[:, n % RING, :], rope_b[:, n % RING, :], part(n, 1), ALU.subtract).then_inc(s_r2, 1)

            dve.wait_ge(s_const, 32)
            for n in range(1, 8 + 3):
                if n <= 8:
                    rope_products(n)
                if n >= 3:
                    second_rest(n - 2)

            def maxima(n, j, tiles):
                past(dve, s_pl, 4 * (n - 1) - 2)
                for i in tiles:
                    dve.wait_ge(s_ms, BT * n + i + 1)
                    dve.tensor_reduce(negmax[:, j % 2, i:i + 1], mbank[:, i % 2, :], AX.X, ALU.max,
                                      negate=True).then_inc(s_mx, 1)

            def finish(n, unit):
                dve.wait_ge(s_ot, n + 1)
                past(dve, s_at, n)
                for qh in range(2):
                    src = bank[7].rearrange("p (b e q c) -> p b q c e", b=4, e=2, q=2)[:, :, qh, 0:HD + 1, :]
                    dve.tensor_reduce(osum[:, qh * 4:(qh + 1) * 4, :], src, AX.X, ALU.add).then_inc(s_oa, 1)
                dve.wait_ge(s_oa, 2 * n + 2)
                dve.reciprocal(orec[:], osum[:, :, HD]).then_inc(s_od, 1)

            def residual(b):
                tl = slice(b * BT, (b + 1) * BT)
                dve.wait_ge(s_at, HEADS * (b + 1))
                link(dve.tensor_tensor(x[:, tl, :].rearrange("p t (h d) -> p t h d", h=HEADS),
                                       x[:, tl, :].rearrange("p t (h d) -> p t h d", h=HEADS),
                                       att[:, b * HEADS:(b + 1) * HEADS, :, :].rearrange("p h t d -> p t h d"), ALU.add))

            maxima(0, 0, range(BT))
            maxima(1, 1, range(BT))

            def body(g, where):
                for j in range(4):
                    n = 4 * g + j
                    ahead = where < 2 or j < 2
                    if ahead:
                        maxima(n + 2, j, range(FINISH))
                    if where > 0 or j > 0:
                        finish(n - 1, n - 1)
                    if where == 2 and j == 0:
                        residual(0)
                    if where == 2 and j == 1 and stage >= 1:
                        layernorm(0, 1)
                    if where == 2 and j == 2 and stage >= 1:
                        normalise(0, 1)
                    if ahead:
                        maxima(n + 2, j, range(FINISH, BT))

            groups(dve, body)
            finish(UNITS - 1, UNITS - 1)
            residual(1)

            def experts(f, k):
                if f == 0:
                    layernorm(1, k)
                    normalise(1, k)
                else:
                    for b in range(BATCH):
                        layernorm(b, k)
                    for b in range(BATCH):
                        normalise(b, k)
                top, total_e, prob, left_of, rank, chosen, place, base, elsewhere = (r8[:, i, :] for i in range(9))
                wide = [P, TILES, EXPERTS]
                dve.wait_ge(s_rt, f + 1)
                logits = bank[4].rearrange("p (c q e) -> p q c e", c=4, q=4)[:, :, :, 0:EXPERTS]
                link(dve.tensor_reduce(top.rearrange("p (q c) -> p q c", q=4), logits, AX.X, ALU.max))
                link_to(dve.tensor_tensor(z_log[:].rearrange("p (q c) e -> p q c e", q=4), logits,
                                          top.rearrange("p (q c) -> p q c", q=4).unsqueeze(3).to_broadcast([P, 4, 4, EXPERTS]),
                                          ALU.subtract), s_zl, f + 1)
                if f == 0:
                    dve.wait_ge(s_moew, 16 * 6)
                leftb = left[:].unsqueeze(1).to_broadcast(wide)
                link(dve.scalar_tensor_tensor(w_log[:], z_log[:], 0.0, leftb, ALU.is_equal, ALU.mult))
                dve.wait_ge(s_el, f + 1)
                dve.tensor_reduce(left_of, w_log[:], AX.X, ALU.max)
                link(dve.tensor_reduce(total_e, e_log[:], AX.X, ALU.add))
                link(dve.reciprocal(prob, total_e))
                for c in range(4):
                    dve.tensor_tensor(diag[:, 4 * c:4 * c + 4, :], ident[:].unsqueeze(1).to_broadcast([P, 4, P]),
                                      prob[:, 4 * c:4 * c + 4].unsqueeze(2).to_broadcast([P, 4, P]), ALU.mult).then_inc(s_dg, 1)
                dve.tensor_tensor(onehot[:], leftb, left_of.unsqueeze(2).to_broadcast(wide), ALU.is_equal).then_inc(s_oh, 1)
                dve.tensor_scalar(elsewhere, left_of, float(EXPERTS), None, ALU.is_lt)
                link(dve.scalar_tensor_tensor(base, left_of, -float(CAP), own_row[:], ALU.mult, ALU.subtract))
                link(dve.tensor_scalar(base, base, float(SLOTS), None, ALU.add))
                if f == 0:
                    dve.tensor_scalar(xn[:, :, D], own_row[:], -float(SLOTS), None, ALU.add)

                def slots(g):
                    tl = slice(4 * g, 4 * g + 4)
                    dve.wait_ge(s_rk, STEPS * f + TILES * (g + 1))
                    link(dve.tensor_tensor(w_log[:, tl, :], bank[g][:, 0:4 * EXPERTS].rearrange("p (t e) -> p t e", t=4),
                                           onehot[:, tl, :], ALU.mult))
                    link(dve.tensor_reduce(rank[:, tl], w_log[:, tl, :], AX.X, ALU.add))
                    dve.scalar_tensor_tensor(chosen[:, tl], rank[:, tl], float(CAP), elsewhere[:, tl], ALU.is_lt, ALU.mult)
                    link(dve.tensor_tensor(place[:, tl], rank[:, tl], base[:, tl], ALU.add))
                    link(dve.tensor_tensor(place[:, tl], place[:, tl], chosen[:, tl], ALU.mult))
                    dve.tensor_tensor(slot[:, tl], place[:, tl], own_row[:, tl], ALU.add).then_inc(s_slot, 1)

                for n in range(STEPS):
                    g, j = n // TILES, n % TILES
                    if j == 0:
                        dve.wait_ge(s_pwc, 4 * f + g + 1)
                    past(dve, s_rk, STEPS * f + max(0, n - RANK_RING + 1))
                    pj = prob[:, j:j + 1]
                    columns = prow[:, g * HALF:(g + 1) * HALF]
                    if j // 4 == g:
                        own = (3 - j % 4) * P
                        ins = dve.scalar_tensor_tensor(before[:, n % RANK_RING, :], columns, pj, tri_tiny[:, own:own + HALF], ALU.subtract, ALU.is_lt)
                    else:
                        ins = dve.tensor_scalar(before[:, n % RANK_RING, :], columns, pj, None, ALU.is_lt if g < j // 4 else ALU.is_le)
                    ins.then_inc(s_bf, 1)
                    if g > 0 and j == 3:
                        slots(g - 1)
                    if n in (20, 43):
                        y_out(f, n // 43)
                slots(3)
                y_out(f, 2)
                y_out(f, 3)
                for e in range(1, EXPERTS):
                    sorted_out(f, e)
                    if e > 1:
                        for i in (1, 3):
                            hidden_out(f, e - 1, i)
                    if e > 2:
                        y_out(f, 3 + e - 2)
                for i in (1, 3):
                    hidden_out(f, EXPERTS - 1, i)
                y_out(f, 3 + EXPERTS - 2)
                y_out(f, 3 + EXPERTS - 1)

            def sorted_out(f, e):
                dve.wait_ge(s_st, (EXPERTS - 1) * f + e)
                dve.tensor_copy(sortedT[:, (e - 1) * CAP:e * CAP], bank[(4, 7)[e % 2]][:, 0:CAP]).then_inc(s_stc, 1)
                dve.wait_ge(s_srt[e], 32 * (f + 1))
                dve.tensor_copy(dest[:, e, 0:2], sorted_x[:, e, 0:2, D])
                dve.tensor_copy(dest[0:CAP - 2 * P, e, 2:3], sorted_x[0:CAP - 2 * P, e, 2, D:ROW]).then_inc(s_dest, 1)

            def add_experts(f, groups_of_tiles):
                for g in groups_of_tiles:
                    dve.wait_ge(s_ga[g], 16 * (f + 1))
                    ins = dve.tensor_tensor(x[:, 4 * g:4 * g + 4, :], x[:, 4 * g:4 * g + 4, :],
                                            gathered[:, 4 * g:4 * g + 4, :], ALU.add)
                link(ins)

            def link_to(ins, semaphore, value):
                ins.then_inc(semaphore, 1)
                dve.wait_ge(semaphore, value)

            def hidden_out(f, e, i):
                h = hs(f, e, i)
                dve.wait_ge(s_h, h + 1)
                dve.wait_ge(s_y, ys(f, 3) if e == 1 else ys(f, 3 + e - 2) + 1)
                dve.tensor_scalar(hidden[:, e % 2, i, 0:CAP], bank[i][:, 0:CAP], b1T[:, e * FT + i:e * FT + i + 1], 0.0,
                                  ALU.add, ALU.max).then_inc(s_hv, 1)

            def y_out(f, i):
                yi = ys(f, i)
                dve.wait_ge(s_y, yi + 1)
                if yi >= 2:
                    dve.wait_ge(*after_store[yi - 2])
                if i < 4:
                    dve.tensor_tensor(y_sb[:, yi % 2, :, :], bank[6].rearrange("p (m d) -> p m d", m=4),
                                      b2[:, 0, :].unsqueeze(1).to_broadcast([P, 4, D]), ALU.add).then_inc(s_yc, 1)
                else:
                    e = i - 3
                    src = bank[5 + e % 2].rearrange("p (m d) -> p m d", m=4)
                    dve.tensor_tensor(y_sb[:, yi % 2, 0:2, :], src[:, 0:2, :],
                                      b2[:, e, :].unsqueeze(1).to_broadcast([P, 2, D]), ALU.add)
                    dve.tensor_tensor(y_sb[0:CAP - 2 * P, yi % 2, 2, :], src[0:CAP - 2 * P, 2, :],
                                      b2[0:CAP - 2 * P, e, :], ALU.add).then_inc(s_yc, 1)

            def softplus():
                v, e, z, z2, p, q = (sp_tmp[:, i, :] for i in range(6))
                by_head = "p (t h) -> p t h"
                dve.wait_ge(m_dt, 1)
                link(dve.tensor_tensor(v.rearrange(by_head, h=SHEADS), bank[4][:, 0:TILES * SHEADS].rearrange(by_head, h=SHEADS),
                                       dt_bias[:].unsqueeze(1).to_broadcast([P, TILES, SHEADS]), ALU.add))
                dve.scalar_tensor_tensor(q, v, -1.0, v, ALU.mult, ALU.min).then_inc(m_dt, 1)
                dve.wait_ge(m_de, 1)
                link(dve.tensor_scalar(z2, e, 2.0, None, ALU.add))
                link(dve.reciprocal(p, z2))
                link(dve.tensor_tensor(z, e, p, ALU.mult))
                link(dve.tensor_tensor(z2, z, z, ALU.mult))
                link(dve.tensor_scalar(p, z2, 1.0 / 17, None, ALU.mult))
                for n in range(15, 1, -2):
                    link(dve.scalar_tensor_tensor(p, p, 1.0 / n, z2, ALU.add, ALU.mult))
                link(dve.scalar_tensor_tensor(q, p, 1.0, z, ALU.add, ALU.mult))
                link(dve.tensor_scalar(q, q, 2.0, None, ALU.mult))
                link(dve.scalar_tensor_tensor(dt[:].rearrange("p t h -> p (t h)"), v, 0.0, q, ALU.max, ALU.add))
                dve.tensor_tensor(log_decay[:], dt[:], neg_a[:].unsqueeze(1).to_broadcast([P, TILES, SHEADS]),
                                  ALU.mult).then_inc(m_dec, 1)

            def state_space(k):
                for b in range(BATCH):
                    add_experts(0, [2 * b, 2 * b + 1])
                    layernorm(b, k)
                for b in range(BATCH):
                    tl = slice(b * BT, (b + 1) * BT)
                    dve.wait_ge(s_rstd, 2 * k + b + 1)
                    link(dve.tensor_tensor(rms[:, tl], meanvar[:, tl, 1], rstd[:, tl], ALU.mult))
                    link(dve.tensor_tensor(rms[:, tl], rms[:, tl], rstd[:, tl], ALU.mult))
                    dve.tensor_scalar(rms[:, tl], rms[:, tl], EPS, None, ALU.add).then_inc(s_ln, 1)
                for b in range(BATCH):
                    for i in range(b * BT, (b + 1) * BT):
                        ins = dve.tensor_scalar(xn[:, i, 0:D], x[:, i, :], meanvar[:, i, 0:1], rstd[:, i:i + 1],
                                                ALU.subtract, ALU.mult)
                    link(ins)
                    dve.wait_ge(s_rstd, 2 * (k + 1) + b + 1)
                    for i in range(b * BT, (b + 1) * BT):
                        ins = dve.tensor_scalar(un[:, i, :], xn[:, i, 0:D], rms[:, i:i + 1], None, ALU.mult)
                    ins.then_inc(s_xn, 1)
                link(dve.tensor_tensor(x[:], x[:], xn[:, :, 0:D], ALU.add))
                dve.wait_ge(s_nega, 1)
                link(dve.tensor_scalar(neg_a[:], neg_a[:], -1.0, None, ALU.mult))
                softplus()
                dve.wait_ge(m_pad, 1)
                for n in range(CONV * BATCH):
                    c, b = n % CONV, n // CONV
                    dve.wait_ge(m_zc, conv_ready(n))
                    past(dve, m_xbc, n - 1)
                    acc = conv_acc[:, n % 2, :]
                    src = before_conv[:, c, b, :]
                    link(dve.tensor_scalar(acc, src[:, 0:SEQ], conv_w[:, c, 0:1], None, ALU.mult))
                    for w in range(1, TAPS):
                        ins = dve.scalar_tensor_tensor(acc, src[:, w:w + SEQ], conv_w[:, c, w:w + 1], acc, ALU.mult, ALU.add)
                        if w < TAPS - 1:
                            link(ins)
                    ins.then_inc(m_conv, 1)

                def chunk_a(i):
                    T, r = chunk_tile(i), i % 2
                    wide = [P, SHEADS, P]
                    thin = [P, SHEADS, SW]
                    dve.wait_ge(m_g, i + 1)
                    dve.tensor_tensor(cb[:, r, :], bank[1][:, 0:P], upto[:], ALU.mult).then_inc(m_gm, 1)
                    dve.wait_ge(m_B, i + 1)
                    past(dve, m_y, i - 1)
                    dve.tensor_tensor(xd[:, r, :, :], bank[0][:, 0:INNER].rearrange("p (h w) -> p h w", h=SHEADS),
                                      dt[:, T, :].unsqueeze(2).to_broadcast(thin), ALU.mult).then_inc(m_xd, 1)
                    dve.wait_ge(m_L, i + 1)
                    dve.wait_ge(m_gm, i + 1)
                    dve.tensor_tensor(mix[:, r, :, :], decay[:, r, :, :], cb[:, r, :].unsqueeze(1).to_broadcast(wide),
                                      ALU.mult).then_inc(m_M, 1)
                    dve.wait_ge(m_xd, i + 1)
                    past(dve, m_s, i - 1)
                    dve.tensor_tensor(xdd[:, r, :, :], xd[:, r, :, :], decay[:, r, :, LAST:P].to_broadcast(thin),
                                      ALU.mult).then_inc(m_xdd, 1)

                def chunk_b(i):
                    T, r, b, c = chunk_tile(i), i % 2, i % 2, i // 2
                    new = bank[5][:, 0:INNER].rearrange("p (h w) -> p h w", h=SHEADS)
                    if c > 0:
                        dve.wait_ge(m_E, i + 1)
                        dve.wait_ge(m_st, i)
                        link(dve.tensor_tensor(st_tmp[:], state[:, b, c % 2, :, :],
                                               from_start[:, r, :, LAST:P].to_broadcast([P, SHEADS, SW]), ALU.mult))
                    dve.wait_ge(m_s, i + 1)
                    past(dve, m_y, i - 1)
                    if c > 0:
                        dve.tensor_tensor(state[:, b, (c + 1) % 2, :, :], new, st_tmp[:], ALU.add).then_inc(m_st, 1)
                    else:
                        dve.tensor_copy(state[:, b, (c + 1) % 2, :, :], new).then_inc(m_st, 1)
                    dve.wait_ge(m_y, i + 1)
                    past(dve, m_yg, i)
                    for ct in range(XC):
                        ins = dve.scalar_tensor_tensor(y_dx[:, ct, :], xbc[:, ct, T * P:(T + 1) * P], d_col[:, ct:ct + 1],
                                                       bank[4][:, ct * P:(ct + 1) * P], ALU.mult, ALU.add)
                    ins.then_inc(m_u, 1)
                    dve.wait_ge(m_u, i + 1)
                    past(dve, m_o, i - 1)
                    past(dve, m_sq, i - 1)
                    dve.tensor_tensor(yg[:, r, :, :], y_dx[:], gate[:, :, T * P:(T + 1) * P], ALU.mult).then_inc(m_yg, 1)

                def chunk_c(i):
                    T = chunk_tile(i)
                    dve.wait_ge(m_o, i + 1)
                    dve.tensor_scalar(ysum[:, T:T + 1], bank[6 + i % 2][:, P:P + 1], 1.0 / INNER, EPS, ALU.mult,
                                      ALU.add).then_inc(m_ms, 1)

                def chunk_d(i):
                    T = chunk_tile(i)
                    dve.wait_ge(m_rs, i + 1)
                    dve.scalar_tensor_tensor(x[:, T, :], bank[6 + i % 2][:, 0:P], ysum[:, T:T + 1], x[:, T, :],
                                             ALU.mult, ALU.add).then_inc(m_fin, 1)

                for i in range(TILES + 3):
                    if i < TILES:
                        chunk_a(i)
                    if 1 <= i <= TILES:
                        chunk_b(i - 1)
                    if i >= 3:
                        chunk_d(i - 3)
                    if 2 <= i < TILES + 2:
                        chunk_c(i - 2)
                dve.wait_ge(m_fin, TILES)

            if stage >= 1:
                experts(0, 1)
            if stage >= 2:
                state_space(2)
            if stage >= 3:
                experts(1, 4)
            if stage == 1 or stage >= 3:
                add_experts(0 if stage == 1 else 1, range(4))
            dve.sem_inc(s_x, 1)

        @block.scalar
        def _(act):
            act.wait_ge(s_wt, 1)
            act.activation(wT[:, 0:4, :], bank[4].rearrange("p (a b) -> p a b", a=4), ACT.Copy).then_inc(s_wtc, 1)
            act.wait_ge(s_wt, 2)
            act.activation(wT[:, 4, :], bank[5][:, 0:P], ACT.Copy).then_inc(s_wtc, 1)

            def transposed(k):
                for i in range(4 * k, 4 * k + 4):
                    act.wait_ge(s_tr, i + 1)
                    act.activation(xnT[:, (i % 4) * HALF:(i % 4 + 1) * HALF], tr_bank(k, i), ACT.Copy).then_inc(s_trc, 1)

            transposed(0)
            for n in range(1, 8 + 3):
                if n <= 8:
                    act.wait_ge(s_rs, n)
                    act.activation(part(n, 0), rope_a[:, n % RING, :], ACT.Copy).then_inc(s_p1, 1)
                if 2 <= n <= 9:
                    act.wait_ge(s_r1, n - 1)
                    act.activation(part(n - 1, 1), rope_b[:, (n - 1) % RING, :], ACT.Copy).then_inc(s_p2, 1)
                if n >= 3:
                    act.wait_ge(s_r2, n - 2)
                    act.activation(part(n - 2, 2), rope_a[:, (n - 2) % RING, :], ACT.Copy).then_inc(s_parts, 1)
            for i in range(TILES // 4):
                act.wait_ge(s_val, i + 1)
                b, t0 = i // 2, 4 * (i % 2)
                act.activation(values[:, b * HEADS:(b + 1) * HEADS, t0:t0 + 4, :].rearrange("p h t d -> p t h d"),
                               bank[4 + i % 2].rearrange("p (t h d) -> p t h d", t=4, h=HEADS), ACT.Copy).then_inc(s_valc, 1)

            def body(g, where):
                for j in range(4):
                    n = 4 * g + j
                    for i in range(16):
                        act.wait_ge(s_sc, 16 * n + i + 1)
                        if i % 4 == 0:
                            past(act, s_pv, 4 * n + i // 4 - 1)
                        act.activation(probs[:, (i // 2) % 4, (i % 2) * HALF:(i % 2 + 1) * HALF], bank[4 + i % 2],
                                       ACT.Exp, scale=ATT_SCALE).then_inc(s_pr, 1)
                        if i == 2 and (where > 0 or j > 0):
                            o_copy(n - 1)
                        if i == ROWS_OUT and (where < 2 or j < 3):
                            rows_out(n + 1, j + 1)

            def rows_out(n, j):
                act.wait_ge(s_mt, n + 1)
                past(act, s_mrow, 16 * PARTS * (n - 1))
                act.activation(maxrows[:, j % 2, :], mtrans, ACT.Copy).then_inc(s_mc, 1)

            rows_out(0, 0)

            def o_copy(n):
                act.wait_ge(s_pv, 4 * (n + 1))
                past(act, s_ot, n)
                act.activation(o_sb[:], bank[6], ACT.Copy).then_inc(s_oc, 1)

            groups(act, body)
            o_copy(UNITS - 1)

            def relu(f, e, i, cols, src, dst):
                h = hs(f, e, i)
                act.wait_ge(s_h, h + 1)
                act.activation(dst, src, ACT.Relu, bias=b1T[:, e * FT + (i % FT):e * FT + (i % FT) + 1]).then_inc(s_ha, 1)

            def experts(f, k):
                if f == 0:
                    act.wait_ge(s_wt, 3)
                    act.activation(routerT[:, 0:EXPERTS], bank[5][:, 0:EXPERTS], ACT.Copy)
                    act.activation(b1T[:], bank[5][:, P:P + EXPERTS * FT], ACT.Copy).then_inc(s_wtc, 1)
                transposed(k)
                act.wait_ge(s_lt, f + 1)
                act.activation(prow[:, 0:HALF], bank[4], ACT.Copy).then_inc(s_lc, 1)
                act.wait_ge(s_zl, f + 1)
                act.activation(e_log[:], z_log[:], ACT.Exp).then_inc(s_el, 1)
                for i in range(16):
                    g = i // FT
                    if i == EARLY:
                        for c in range(4):
                            act.wait_ge(s_pw, 4 * f + c + 1)
                            act.activation(prow[:, c * HALF:(c + 1) * HALF], bank[c], ACT.Copy).then_inc(s_pwc, 1)
                    if g >= 2 and i % FT == 0:
                        act.wait_ge(s_y, ys(f, g - 2) + 1)
                    relu(f, 0, i, HALF, bank[(5, 7)[i % 2]], hidden[:, g % 2, i % FT, :])
                for e in range(1, EXPERTS):
                    for i in (0, 2):
                        if e == 1:
                            act.wait_ge(s_y, ys(f, 3))
                        else:
                            act.wait_ge(s_y, ys(f, 3 + e - 2) + 1)
                        relu(f, e, i, CAP, bank[i][:, 0:CAP], hidden[:, e % 2, i, 0:CAP])

            def state_space(kt):
                act.wait_ge(m_w, 16 * 15)
                act.activation(neg_a[:], a_log[:], ACT.Exp).then_inc(s_nega, 1)
                for j in range(3):
                    act.wait_ge(m_wt, j + 1)
                    if j < 2:
                        n = (4 * P, 2 * P + SHEADS)[j]
                        act.activation(winT[:, 4 * j * P:4 * j * P + n], bank[j][:, 0:n], ACT.Copy, scale=norm_w[:, 0:1]).then_inc(m_wc, 1)
                    else:
                        for c in range(XC):
                            act.activation(woutT[:, c, :], bank[2][:, c * P:(c + 1) * P], ACT.Copy,
                                           scale=gnorm_w[:, c:c + 1]).then_inc(m_wc, 1)
                transposed(kt)
                act.wait_ge(m_dt, 2)
                act.activation(sp_tmp[:, 1, :], sp_tmp[:, 5, :], ACT.Exp).then_inc(m_de, 1)
                done = 0
                for n in range(24):
                    g, j = n // 6, n % 6
                    act.wait_ge(m_zx, n + 1)
                    if j < CONV:
                        act.activation(before_conv[:, j, g // 2, TAPS - 1 + (g % 2) * HALF:TAPS - 1 + (g % 2 + 1) * HALF],
                                       bank[n % 4], ACT.Copy).then_inc(m_zc, 1)
                    else:
                        act.activation(gate[:, j - CONV, g * HALF:(g + 1) * HALF], bank[n % 4], ACT.Silu).then_inc(m_zc, 1)
                for n in range(CONV * BATCH):
                    c, b = n % CONV, n // CONV
                    act.wait_ge(m_conv, n + 1)
                    act.activation(xbc[:, c, b * SEQ:(b + 1) * SEQ], conv_acc[:, n % 2, :], ACT.Silu,
                                   bias=conv_b[:, c:c + 1]).then_inc(m_xbc, 1)
                for i in range(TILES + 1):
                    r = i % 2
                    if i < TILES:
                        act.wait_ge(m_tp, i + 1)
                        past(act, m_s, i - 1)
                        act.activation(b_tok[:, r, :], bank[0][:, INNER:INNER + STATE], ACT.Copy).then_inc(m_B, 1)
                        act.wait_ge(m_df, i + 1)
                        past(act, m_xdd, i - 1)
                        act.activation(decay[:, r, :, :].rearrange("p h n -> p (h n)"), bank[2], ACT.Exp).then_inc(m_L, 1)
                        act.wait_ge(m_bc, i + 1)
                        past(act, m_CE, i - 1)
                        past(act, m_st, i - 1)
                        act.activation(from_start[:, r, :, :].rearrange("p h n -> p (h n)"), bank[3], ACT.Exp).then_inc(m_E, 1)
                    if i >= 1:
                        act.wait_ge(m_yg, i)
                        past(act, m_o, i - 2)
                        act.activation(ysq[:, (i - 1) % 2, :, :], yg[:, (i - 1) % 2, :, :], ACT.Square).then_inc(m_sq, 1)

            if stage >= 1:
                experts(0, 1)
            if stage >= 2:
                state_space(2)
            if stage >= 3:
                experts(1, 3)
            act.wait_ge(s_x, 1)
            act.dma_start(out.rearrange("b (t p) d -> p (b t) d", p=P), x[:]).then_inc(s_out, 16)

        @block.tensor
        def _(pe):
            pe.wait_ge(s_w, 80)
            for i in range(3):
                pe.matmul(bank[4][:, i * P:(i + 1) * P], wqkv[:, i, :], ident[:], start=True, stop=True)
            pe.matmul(bank[4][:, 3 * P:4 * P], wqkv[:, 0, :], rot[:], start=True, stop=True).then_inc(s_wt, 1)
            pe.matmul(bank[5][:, 0:P], wqkv[:, 1, :], rot[:], start=True, stop=True).then_inc(s_wt, 1)

            def transpose_tiles(k, src):
                for i in range(4):
                    pe.wait_ge(s_xn, 2 * k + i // 2 + 1)
                    past(pe, s_trc, 4 * k + i - 1)
                    for c in range(4):
                        ins = pe.transpose(tr_bank(k, i)[:, c * P:(c + 1) * P], src[:, 4 * i + c, 0:D], ident[:])
                    ins.then_inc(s_tr, 1)

            transpose_tiles(0, xn)
            n = 0
            pe.wait_ge(s_wtc, 2)
            for b in range(BATCH):
                for side in range(2):
                    for h in range(2):
                        n += 1
                        pe.wait_ge(s_trc, 2 * b + h + 1)
                        past(pe, s_projc, n - 2)
                        rhs = xnT[:, b * SEQ + h * HALF:b * SEQ + (h + 1) * HALF]
                        pe.matmul(bank[(2 * n) % 4], wT[:, side, :], rhs, start=True, stop=True)
                        pe.matmul(bank[(2 * n + 1) % 4], wT[:, 3 + side, :], rhs, start=True, stop=True).then_inc(s_proj, 1)
            for i in range(TILES // 4):
                past(pe, s_valc, i - 1)
                for k in range(4):
                    ins = pe.matmul(bank[4 + i % 2][:, k * P:(k + 1) * P], xnT[:, (4 * i + k) * P:(4 * i + k + 1) * P],
                                    wT[:, 2, :], start=True, stop=True)
                ins.then_inc(s_val, 1)
            pe.wait_ge(s_valc, TILES // 4)
            pe.wait_ge(s_projc, 8)
            pe.wait_ge(s_init, 2)
            pe.wait_ge(s_id16, 1)

            def max_scores(n, slot, i, load_turn):
                if i == 0:
                    pe.wait_ge(s_load[slot], LOADS * 16 * (load_turn + 1))
                past(pe, s_mx, BT * n + i - 1)
                for h in range(2):
                    ins = pe.matmul(bank[2 * (i % 2) + h], qa[0:KROWS, slot, i * P:(i + 1) * P],
                                    ka[0:KROWS, slot, h * HALF:(h + 1) * HALF], start=True, stop=True)
                ins.then_inc(s_ms, 1)

            def max_transpose(n):
                pe.wait_ge(s_mp, n + 1)
                past(pe, s_oa, 2 * (n - 2))
                pe.transpose(mtrans, maxparts[:].rearrange("p a t -> p (a t)"), ident16[:]).then_inc(s_mt, 1)

            def scores(n, slot, i):
                if i == 0:
                    pe.wait_ge(s_mrow, 16 * PARTS * (n + 1))
                past(pe, s_pr, 16 * n + i - 1)
                pe.matmul(bank[4 + i % 2], ka[0:KROWS + PARTS, slot, (i // 2) * P:(i // 2 + 1) * P],
                          qa[0:KROWS + PARTS, slot, (i % 2) * HALF:(i % 2 + 1) * HALF], start=True, stop=True).then_inc(s_sc, 1)

            def values_product(n, vslot, k):
                if k == 0:
                    pe.wait_ge(s_vst, n + 1)
                    past(pe, s_oc, n)
                pe.wait_ge(s_pr, 16 * n + 4 * k + 4)
                for e in range(2):
                    for h in range(2):
                        q = VCOL * (2 * e + h)
                        ins = pe.matmul(bank[6][q:q + VCOL, :], vstage[:, vslot, 2 * k + e, :],
                                        probs[:, (2 * k + e) % 4, h * HALF:(h + 1) * HALF],
                                        start=(k == 0), stop=(k == 3))
                ins.then_inc(s_pv, 1)

            def out_transpose(n, maxima_out):
                pe.wait_ge(s_oc, n + 1)
                past(pe, s_oa, 2 * n)
                pe.wait_ge(s_mc, maxima_out)
                for k in range(4):
                    ins = pe.transpose(bank[7][:, k * P:(k + 1) * P], o_sb[:, k * P:(k + 1) * P], ident[:])
                ins.then_inc(s_ot, 1)

            for i in range(BT):
                max_scores(0, 0, i, 0)
            max_transpose(0)
            for i in range(BT):
                max_scores(1, 1, i, 0)

            def body(g, where):
                for j in range(4):
                    n = 4 * g + j
                    ahead = where < 2 or j < 2
                    turn = g + (j + 2) // 4
                    for k in range(4):
                        scores(n, j, 4 * k)
                        scores(n, j, 4 * k + 1)
                        if k > 0:
                            values_product(n, j % 2, k - 1)
                        elif where > 0 or j > 0:
                            values_product(n - 1, (j + 1) % 2, 3)
                        scores(n, j, 4 * k + 2)
                        scores(n, j, 4 * k + 3)
                        if ahead:
                            max_scores(n + 2, (j + 2) % 4, 2 * k, turn)
                            max_scores(n + 2, (j + 2) % 4, 2 * k + 1, turn)
                        if k == 1 and (where < 2 or j < 3):
                            max_transpose(n + 1)
                        if k == 2 and (where > 0 or j > 0):
                            out_transpose(n - 1, n + 2 if where < 2 or j < 3 else UNITS)

            groups(pe, body)
            values_product(UNITS - 1, 1, 3)
            out_transpose(UNITS - 1, UNITS)

            def experts(f, k):
                if f == 0:
                    pe.wait_ge(s_moew, 16 * 6)
                    pe.transpose(bank[5][:, 0:EXPERTS], router[:], ident[0:EXPERTS, 0:EXPERTS])
                    pe.transpose(bank[5][:, P:P + EXPERTS * FT], b1rows[:], ident[0:EXPERTS * FT, 0:EXPERTS * FT]).then_inc(s_wt, 1)
                transpose_tiles(k, xn)
                pe.wait_ge(s_wtc, 3)
                for q in range(4):
                    pe.wait_ge(s_trc, 4 * k + q + 1)
                    ins = pe.matmul(bank[4][q * QUAD:(q + 1) * QUAD, :], routerT[:], xnT[:, q * HALF:(q + 1) * HALF],
                                    start=True, stop=True)
                ins.then_inc(s_lt, 1)
                pe.wait_ge(s_lc, f + 1)
                for c in range(4):
                    ins = pe.transpose(bank[4][:, c * P:(c + 1) * P], prow[:, c * P:(c + 1) * P], ident[:])
                ins.then_inc(s_rt, 1)
                pe.wait_ge(s_ew, 32 * EXPERTS)


                def dense_hidden(i):
                    h = hs(f, 0, i)
                    if i >= 2:
                        pe.wait_ge(s_ha, acts(f) + i - 1)
                    pe.matmul(bank[(5, 7)[i % 2]], w1[:, 0, (i % FT) * P:(i % FT + 1) * P],
                              xnT[:, (i // FT) * HALF:(i // FT + 1) * HALF], start=True, stop=True).then_inc(s_h, 1)

                def dense_out(i):
                    g = i // 4
                    pe.wait_ge(s_ha, acts(f) + 4 * g + 4)
                    if i % 4 == 0:
                        past(pe, s_yc, ys(f, g))
                    for c in range(FT):
                        ins = pe.matmul(bank[6][:, (i % 4) * D:(i % 4 + 1) * D],
                                        hidden[:, g % 2, c, (i % 4) * P:(i % 4 + 1) * P], w2[:, 0, c, :],
                                        start=(c == 0), stop=(c == FT - 1))
                    if i % 4 == 3:
                        ins.then_inc(s_y, 1)

                dense = ([(dense_hidden, i) for i in range(2 * FT)] + [(dense_out, i) for i in range(4)] +
                         [(dense_hidden, i) for i in range(2 * FT, 3 * FT)] + [(dense_out, i) for i in range(4, 8)] +
                         [(dense_hidden, i) for i in range(3 * FT, 4 * FT)] + [(dense_out, i) for i in range(8, 16)])
                for step, i in dense[:EARLY]:
                    step(i)
                for c in range(4):
                    pe.wait_ge(s_dg, 4 * f + c + 1)
                    pe.matmul(bank[c], ones[:], diag[:, 4 * c:4 * c + 4, :].rearrange("p t n -> p (t n)"),
                              start=True, stop=True).then_inc(s_pw, 1)
                pe.wait_ge(s_oh, f + 1)
                for n in range(STEPS):
                    g, j = n // TILES, n % TILES
                    if j == 0:
                        pe.wait_ge(s_pwc, 4 * f + g + 1)
                    pe.wait_ge(s_bf, STEPS * f + n + 1)
                    for i in range(4):
                        ins = pe.matmul(bank[g][:, i * EXPERTS:(i + 1) * EXPERTS], before[:, n % RANK_RING, i * P:(i + 1) * P],
                                        onehot[:, j, :], start=(j == 0 and i == 0), stop=(j == TILES - 1),
                                        skip_group_check=True)
                    ins.then_inc(s_rk, 1)
                    if n % 3 == 2:
                        step, i = dense[EARLY + n // 3]
                        step(i)
                for step, i in dense[EARLY + STEPS // 3:]:
                    step(i)

                def sorted_in(e):
                    pe.wait_ge(s_srt[e], 32 * (f + 1))
                    if e == 1:
                        pe.wait_ge(s_ha, acts(f) + 16)
                    elif e > 2:
                        pe.wait_ge(s_stc, (EXPERTS - 1) * f + e - 2)
                    for m in range(CT):
                        n = min(P, CAP - m * P)
                        ins = pe.transpose(bank[(4, 7)[e % 2]][:, m * P:m * P + n], sorted_x[0:n, e, m, 0:D], ident[0:n, 0:n])
                    ins.then_inc(s_st, 1)

                def sparse_hidden(e):
                    pe.wait_ge(s_stc, (EXPERTS - 1) * f + e)
                    if e == 1:
                        pe.wait_ge(s_slot, 4 * f + 4)
                    for i in range(FT):
                        if e > 1:
                            if i % 2 == 0:
                                pe.wait_ge(s_ha, acts(f) + 16 + 2 * (e - 2) + i // 2 + 1)
                            else:
                                pe.wait_ge(s_hv, 2 * (EXPERTS - 1) * f + 2 * (e - 2) + i // 2 + 1)
                        pe.matmul(bank[i][:, 0:CAP], w1[:, e, i * P:(i + 1) * P], sortedT[:, (e - 1) * CAP:e * CAP],
                                  start=True, stop=True).then_inc(s_h, 1)

                def sparse_out(e):
                    pe.wait_ge(s_ha, acts(f) + 16 + 2 * e)
                    pe.wait_ge(s_hv, 2 * (EXPERTS - 1) * f + 2 * e)
                    pe.wait_ge(s_yc, ys(f, 3 + e - 2) + 1 if e > 1 else ys(f, 3) + 1)
                    for m in range(CT):
                        n = min(P, CAP - m * P)
                        for c in range(FT):
                            ins = pe.matmul(bank[5 + e % 2][0:n, m * D:(m + 1) * D], hidden[:, e % 2, c, m * P:m * P + n],
                                            w2[:, e, c, :], start=(c == 0), stop=(c == FT - 1))
                    ins.then_inc(s_y, 1)

                sorted_in(1)
                sorted_in(2)
                sparse_hidden(1)
                for e in range(1, EXPERTS):
                    if e < EXPERTS - 1:
                        sparse_hidden(e + 1)
                    if e < EXPERTS - 2:
                        sorted_in(e + 2)
                    sparse_out(e)

            def state_space(kt):
                pe.wait_ge(m_w, 16 * 15)
                for c in range(6):
                    ins = pe.transpose(bank[c // 4][:, (c % 4) * P:(c % 4 + 1) * P], win_rows[:, c, :], ident[:])
                    if c == 3:
                        ins.then_inc(m_wt, 1)
                pe.transpose(bank[1][:, 2 * P:2 * P + SHEADS], wdt_rows[:], ident[0:SHEADS, 0:SHEADS]).then_inc(m_wt, 1)
                for c in range(XC):
                    ins = pe.transpose(bank[2][:, c * P:(c + 1) * P], wout_rows[:, c * P:(c + 1) * P], ident[:])
                ins.then_inc(m_wt, 1)
                transpose_tiles(kt, un)
                pe.wait_ge(m_wc, 4)
                pe.wait_ge(s_trc, 4 * kt + 4)
                for i in range(TILES):
                    ins = pe.matmul(bank[4][:, i * SHEADS:(i + 1) * SHEADS], xnT[:, i * P:(i + 1) * P], winT[:, 6 * P:6 * P + SHEADS],
                                    start=True, stop=True)
                ins.then_inc(m_dt, 1)
                for n in range(24):
                    g, j = n // 6, n % 6
                    c = XC + j if j < CONV else j - CONV
                    past(pe, m_zc, n - 3)
                    pe.matmul(bank[n % 4], winT[:, c * P:(c + 1) * P], xnT[:, g * HALF:(g + 1) * HALF],
                              start=True, stop=True).then_inc(m_zx, 1)
                pe.wait_ge(m_zc, 24)
                pe.wait_ge(m_dec, 1)
                pe.wait_ge(m_xbc, CONV * BATCH)

                def chunk_a(i):
                    T = chunk_tile(i)
                    cols = slice(T * P, (T + 1) * P)
                    past(pe, m_xd, i)
                    past(pe, m_B, i)
                    for c in range(XC + 1):
                        ins = pe.transpose(bank[0][:, c * P:(c + 1) * P], xbc[:, c, cols], ident[:])
                    ins.then_inc(m_tp, 1)
                    past(pe, m_gm, i)
                    pe.matmul(bank[1][:, 0:P], xbc[:, XC, cols], xbc[:, XC + 1, cols], start=True, stop=True).then_inc(m_g, 1)
                    pe.wait_ge(m_ua, i + 1)
                    past(pe, m_L, i)
                    for h in range(SHEADS):
                        ins = pe.matmul(bank[2][:, h * P:(h + 1) * P], seg[:, i % 2, h, :], upto[:], start=True, stop=True)
                    ins.then_inc(m_df, 1)
                    past(pe, m_E, i)
                    for h in range(SHEADS):
                        ins = pe.matmul(bank[3][:, h * P:(h + 1) * P], log_decay[:, T, h:h + 1].to_broadcast([P, P]), upto[:],
                                        start=True, stop=True)
                    ins.then_inc(m_bc, 1)

                def chunk_b(i):
                    r, b, c = i % 2, i % 2, i // 2
                    pe.wait_ge(m_M, i + 1)
                    pe.wait_ge(m_CE, i + 1)
                    pe.wait_ge(m_xd, i + 1)
                    past(pe, m_st, i - 1)
                    past(pe, m_u, i)
                    for h in range(SHEADS):
                        dst = bank[4][(h % 2) * SW:(h % 2 + 1) * SW, (h // 2) * P:(h // 2 + 1) * P]
                        ins = pe.matmul(dst, xd[:, r, h, :], mix[:, r, h, :], start=True, stop=(c == 0))
                        if c > 0:
                            ins = pe.matmul(dst, state[:, b, c % 2, h, :], c_dec[:, r, h, :], start=False, stop=True)
                    ins.then_inc(m_y, 1)
                    pe.wait_ge(m_B, i + 1)
                    pe.wait_ge(m_xdd, i + 1)
                    past(pe, m_st, i)
                    pe.matmul(bank[5][:, 0:INNER], b_tok[:, r, :], xdd[:, r, :, :].rearrange("p h w -> p (h w)"),
                              start=True, stop=True).then_inc(m_s, 1)

                def chunk_c(i):
                    r = i % 2
                    pe.wait_ge(m_sq, i + 1)
                    past(pe, m_fin, i - 1)
                    for c in range(XC):
                        pe.matmul(bank[6 + r][:, P:2 * P], ysq[:, r, c, :], ones[:], start=(c == 0), stop=(c == XC - 1))
                    for c in range(XC):
                        ins = pe.matmul(bank[6 + r][:, 0:P], yg[:, r, c, :], woutT[:, c, :], start=(c == 0), stop=(c == XC - 1))
                    ins.then_inc(m_o, 1)

                for i in range(TILES + 2):
                    if i < TILES:
                        chunk_a(i)
                    if 1 <= i <= TILES:
                        chunk_b(i - 1)
                    if i >= 2:
                        chunk_c(i - 2)

            if stage >= 1:
                experts(0, 1)
            if stage >= 2:
                state_space(2)
            if stage >= 3:
                experts(1, 3)


def shape_constants():
    import numpy as np
    c = {}
    c["ident"] = np.eye(P, dtype=np.float32)
    rot = np.zeros((P, P), np.float32)
    for i in range(0, P, 2):
        rot[i + 1, i] = -1.0
        rot[i, i + 1] = 1.0
    c["rot"] = rot
    row, col = np.arange(P)[:, None], np.arange(P)[None, :]
    c["after"] = (row > col).astype(np.float32)
    c["upto"] = (row <= col).astype(np.float32)
    c["left"] = np.tile(EXPERTS - np.arange(EXPERTS, dtype=np.float32), (P, 1))
    c["own_row"] = (SLOTS + np.arange(TOK, dtype=np.float32)).reshape(TILES, P).T.copy()
    c["tri_tiny"] = np.where(np.arange(P)[:, None] < np.arange(7 * P)[None, :] - 3 * P, np.float32(TINY), np.float32(0)).astype(np.float32)
    c["spare_row"] = (TOK + np.arange(SLOTS, dtype=np.float32)).reshape(SLOTS, 1)
    inv = (np.float32(1.0) / np.float32(10000.0) ** (np.arange(0, HD, 2, dtype=np.float32) / np.float32(HD))).astype(np.float32)
    ang = np.outer(np.arange(SEQ, dtype=np.float32), inv).astype(np.float32)
    rows = (np.arange(P) % HD) // 2
    c["cos"] = np.ascontiguousarray(np.cos(ang).astype(np.float32).T[rows])
    c["sin"] = np.ascontiguousarray(np.sin(ang).astype(np.float32).T[rows])
    return c


_INS = ['L0_attn_a_x', 'L0_attn_a_wq', 'L0_attn_a_wk', 'L0_attn_a_wv', 'L0_attn_b_norm_w', 'L0_attn_b_in_proj_w',
        'L0_attn_b_conv_w', 'L0_attn_b_conv_b', 'L0_attn_b_dt_bias', 'L0_attn_b_A_log', 'L0_attn_b_D',
        'L0_attn_b_gnorm_w', 'L0_attn_b_out_proj_w', 'L0_ffn_router_w', 'L0_ffn_W1', 'L0_ffn_b1', 'L0_ffn_W2',
        'L0_ffn_b2']


def kernel(**inputs):
    import numpy as _np
    import concourse.bacc as _bacc
    from concourse import mybir as _mybir
    from concourse.bass_utils import run_bass_kernel_spmd as _run

    nc = _bacc.Bacc("TRN2", target_bir_lowering=False, num_devices=1)
    arrays, tensors = {}, {}
    for name, a in [(n, inputs[n]) for n in _INS] + list(shape_constants().items()):
        a = _np.ascontiguousarray(a)
        arrays[f"in_{name}_dram"] = a
        tensors[name] = nc.dram_tensor(f"in_{name}_dram", a.shape, _mybir.dt.from_np(a.dtype), kind="ExternalInput").ap()
    out = nc.dram_tensor("out_0_dram", (BATCH, SEQ, D), _mybir.dt.float32, kind="ExternalOutput").ap()
    bass_hybrid(nc, tensors, out)
    r = _run(nc, [arrays], core_ids=[0])
    return r.results[0]["out_0_dram"]
```

```python
from contextlib import ExitStack

import concourse.bass as bass
from concourse import mybir

F32 = mybir.dt.float32
BF16 = mybir.dt.bfloat16
U32 = mybir.dt.uint32
ALU = mybir.AluOpType
ACT = mybir.ActivationFunctionType
AX = mybir.AxisListType

P = 128
BATCH, SEQ, D = 2, 1024, 128
TOK = BATCH * SEQ
TILES = TOK // P
BT = SEQ // P
HEADS, HD = 16, 8
UNITS = BATCH * HEADS
EPS = 1e-5
EXPERTS, FF = 8, 512
FT = FF // P
CAP = 320
CT = 3
SLOTS = (EXPERTS - 1) * CAP
ROWS = SLOTS + TOK
ROW = D + 1
FILL = 112
QUAD = 32
EARLY = 3
OUT_STEPS = (29, 53)
STEPS = 4 * TILES
RANK_RING = 6
INNER, STATE, TAPS = 256, 128, 4
SHEADS, SW = 4, 64
XC = INNER // P
CONV = XC + 2
PROJ = 2 * INNER + 2 * STATE + SHEADS
LAST = P - 1
TINY = 1e-9
PARTS = 3
SROWS = PARTS * PARTS * HD
KROWS = 96
ATT_SCALE = float(HD) ** -0.5
FINISH = 5
ROWS_OUT = 9
RING = 4
LOADS = PARTS + 1
HALF = 512
VCOL = 32
UCOL = HD + 1
PAIRS = UNITS // 2


def bass_hybrid(nc, t, out, stage=9):
    ctx = ExitStack()
    with ctx:
        def sb(name, shape, dt=F32):
            return ctx.enter_context(nc.sbuf_tensor(name, shape, dt))

        def pb(name, shape, dt=F32):
            return ctx.enter_context(nc.psum_tensor(name, shape, dt))

        def sem(name):
            return ctx.enter_context(nc.semaphore(name))

        def dram(name, shape, dt=F32):
            return nc.dram_tensor(name, shape, dt, kind="Internal").ap()

        qparts_dram = dram("qparts_dram", [UNITS, PARTS, HD, SEQ], BF16)
        kparts_dram = dram("kparts_dram", [UNITS, PARTS, HD, SEQ], BF16)

        sorted_dram = [dram(f"sorted_dram{f}", [ROWS, ROW]) for f in range(2)]
        y_dram = [dram(f"y_dram{f}", [TOK + SLOTS, D]) for f in range(2)]

        x = sb("x", [P, TILES, D])
        xn = sb("xn", [P, TILES, ROW])
        xnT = sb("xnT", [P, TOK])
        stats = sb("stats", [P, TILES, 6])
        meanvar = sb("meanvar", [P, TILES, 2])
        rstd = sb("rstd", [P, TILES])
        neghalf = sb("neghalf", [P, TILES])
        ident = sb("ident", [P, P])
        ident16 = sb("ident16", [P, P], BF16)

        w1 = sb("w1", [P, EXPERTS, FF])
        w2 = sb("w2", [P, EXPERTS, FT, D])
        b1T = sb("b1T", [P, EXPERTS * FT])
        b1rows = sb("b1rows", [EXPERTS * FT, P])
        b2 = sb("b2", [P, EXPERTS, D])
        router = sb("router", [EXPERTS, D])
        routerT = sb("routerT", [P, QUAD])
        left = sb("left", [P, EXPERTS])
        own_row = sb("own_row", [P, TILES])
        tri_tiny = sb("tri_tiny", [P, 7 * P])
        ones = sb("ones", [P, P])
        zeros = sb("zeros", [P, D])
        z_log = sb("z_log", [P, TILES, EXPERTS])
        e_log = sb("e_log", [P, TILES, EXPERTS])
        w_log = sb("w_log", [P, TILES, EXPERTS])
        onehot = sb("onehot", [P, TILES, EXPERTS], BF16)
        r8 = sb("r8", [P, 9, TILES])
        slot = sb("slot", [P, TILES], U32)

        win_rows = sb("win_rows", [P, 6, P])
        wdt_rows = sb("wdt_rows", [SHEADS, P])
        wout_rows = sb("wout_rows", [P, INNER])
        winT = sb("winT", [P, 6 * P])
        wdtT = sb("wdtT", [P, QUAD])
        woutT = sb("woutT", [P, XC, D])
        norm_w = sb("norm_w", [P, 1])
        gnorm_w = sb("gnorm_w", [P, XC])
        conv_w = sb("conv_w", [P, CONV, TAPS])
        conv_b = sb("conv_b", [P, CONV])
        d_col = sb("d_col", [P, XC])
        dt_bias = sb("dt_bias", [P, SHEADS])
        a_log = sb("a_log", [P, SHEADS])
        neg_a = sb("neg_a", [P, SHEADS])
        after = sb("after", [P, P])
        upto = sb("upto", [P, P])
        dt = sb("dt", [P, TILES, SHEADS])
        log_decay = sb("log_decay", [P, TILES, SHEADS])
        sp_tmp = sb("sp_tmp", [P, 6, TILES * SHEADS])
        rms = sb("rms", [P, TILES])
        ysum = sb("ysum", [P, TILES])

        scope = ExitStack()

        def sb(name, shape, dt=F32):
            return scope.enter_context(nc.sbuf_tensor(name, shape, dt))

        rot = sb("rot", [P, P])
        cosT = sb("cosT", [P, SEQ])
        sinT = sb("sinT", [P, SEQ])
        wqkv = sb("wqkv", [P, 3, P])
        wT = sb("wT", [P, 5, P])
        rope_a = sb("rope_a", [P, RING, HALF])
        rope_b = sb("rope_b", [P, RING, HALF])
        parts16 = sb("parts16", [P, 2, PARTS, TOK], BF16)
        values = sb("values", [P, UNITS, BT, HD])
        vstage = sb("vstage", [P, 2, BT, VCOL])
        qa = sb("qa", [P, 4, SEQ], BF16)
        ka = sb("ka", [P, 4, SEQ], BF16)
        negmax = sb("negmax", [P, 2, BT])
        maxrest = sb("maxrest", [P, 2, BT])
        maxparts = sb("maxparts", [P, PARTS, BT], BF16)
        maxrows = sb("maxrows", [PARTS * BT, 2, P], BF16)
        probs = sb("probs", [P, 4, SEQ])
        o_sb = sb("o_sb", [P, HALF])
        osum = sb("osum", [P, BT, 2 * UCOL])
        orec = sb("orec", [P, BT, 2])
        att = sb("att", [P, UNITS, BT, HD])

        scope.close()
        diag = sb("diag", [P, TILES, P])
        prow = sb("prow", [P, TOK])
        before = sb("before", [P, RANK_RING, HALF], BF16)
        hidden = sb("hidden", [P, 2, FT, HALF])
        y_sb = sb("y_sb", [P, 2, 4, D])
        sorted_x = sb("sorted_x", [P, EXPERTS, CT, ROW])
        dest = sb("dest", [P, EXPERTS, CT], U32)
        sortedT = sb("sortedT", [P, SLOTS])
        gathered = sb("gathered", [P, TILES, D])
        scope.close()
        before_conv = sb("before_conv", [P, CONV, BATCH, TAPS - 1 + SEQ])
        xbc = sb("xbc", [P, CONV, TOK])
        gate = sb("gate", [P, XC, TOK])
        un = gate[:, 0, :].rearrange("p (t d) -> p t d", t=TILES)
        seg = sb("seg", [P, 2, SHEADS, P])
        decay = sb("decay", [P, 2, SHEADS, P])
        grown = sb("grown", [P, 2, TILES, SHEADS])
        y_before = sb("y_before", [P, 2, SHEADS, SW])
        b_tok = sb("b_tok", [P, 2, STATE])
        cb = sb("cb", [P, 2, P])
        mix = sb("mix", [P, 2, SHEADS, P])
        xd = sb("xd", [P, 2, SHEADS, SW])
        xdd = sb("xdd", [P, 2, SHEADS, SW])
        state = sb("state", [P, BATCH, 2, SHEADS, SW])
        st_tmp = sb("st_tmp", [P, 2, SHEADS, SW])
        y_dx = sb("y_dx", [P, XC, P])
        dtT = sb("dtT", [P, HALF])
        yg = sb("yg", [P, 3, XC, P])
        ysq = sb("ysq", [P, 3, XC, P])
        scope.close()

        mbank = pb("mbank", [P, 2, SEQ])
        ebank = pb("ebank", [P, 2, HALF])
        obank = pb("obank", [P, HALF])
        tbank = pb("tbank", [P, HALF])
        mtrans = tbank[:].bitcast(BF16)[0:PARTS * BT, 0:P]
        bank = [mbank[:, 0, 0:HALF], mbank[:, 0, HALF:SEQ], mbank[:, 1, 0:HALF], mbank[:, 1, HALF:SEQ],
                ebank[:, 0, :], ebank[:, 1, :], obank[:], tbank[:]]

        s_const = sem("s_const")
        s_w = sem("s_w")
        s_x = sem("s_x")
        s_xin = [sem(f"s_xin{b}") for b in range(BATCH)]
        s_init = sem("s_init")
        s_ones = sem("s_ones")
        s_id16 = sem("s_id16")
        s_dve = sem("s_dve")
        s_ln = sem("s_ln")
        s_rstd = sem("s_rstd")
        s_pool = sem("s_pool")
        s_xn = sem("s_xn")
        s_tr = sem("s_tr")
        s_trc = sem("s_trc")
        s_wt = sem("s_wt")
        s_wtc = sem("s_wtc")
        s_proj = sem("s_proj")
        s_projc = sem("s_projc")
        s_val = sem("s_val")
        s_valc = sem("s_valc")
        s_rs = sem("s_rs")
        s_p1 = sem("s_p1")
        s_r1 = sem("s_r1")
        s_p2 = sem("s_p2")
        s_r2 = sem("s_r2")
        s_parts = sem("s_parts")
        s_pl = sem("s_pl")
        s_pstore = [sem(f"s_pstore{b}") for b in range(BATCH)]
        s_load = [sem(f"s_load{i}") for i in range(4)]
        s_vst = sem("s_vst")
        s_ms = sem("s_ms")
        s_mx = sem("s_mx")
        s_mp = sem("s_mp")
        s_mt = sem("s_mt")
        s_mc = sem("s_mc")
        s_mrow = sem("s_mrow")
        s_sc = sem("s_sc")
        s_pr = sem("s_pr")
        s_pv = sem("s_pv")
        s_oc = sem("s_oc")
        s_ot = sem("s_ot")
        s_od = sem("s_od")
        s_at = sem("s_at")
        s_oa = sem("s_oa")
        s_zero = sem("s_zero")
        s_moew = sem("s_moew")
        s_ew = sem("s_ew")
        s_rt = sem("s_rt")
        s_zl = sem("s_zl")
        s_el = sem("s_el")
        s_oh = sem("s_oh")
        s_dg = sem("s_dg")
        s_pw = sem("s_pw")
        s_pwc = sem("s_pwc")
        s_bf = sem("s_bf")
        s_lt = sem("s_lt")
        s_lc = sem("s_lc")
        s_rk = sem("s_rk")
        s_slot = sem("s_slot")
        s_scat = sem("s_scat")
        s_srt = [sem(f"s_srt{i}") for i in range(EXPERTS)]
        s_dest = sem("s_dest")
        s_st = sem("s_st")
        s_stc = sem("s_stc")
        s_h = sem("s_h")
        s_ha = sem("s_ha")
        s_hv = sem("s_hv")
        s_y = sem("s_y")
        s_yc = sem("s_yc")
        s_yst = [sem(f"s_yst{i}") for i in range(2)]
        s_ysc = [sem(f"s_ysc{i}") for i in range(2)]
        s_ga = [sem(f"s_ga{i}") for i in range(4)]
        s_out = sem("s_out")
        m_w = sem("m_w")
        s_nega = sem("s_nega")
        m_wt = sem("m_wt")
        m_wc = sem("m_wc")
        m_pad = sem("m_pad")
        m_zx = sem("m_zx")
        m_zc = sem("m_zc")
        m_conv = sem("m_conv")
        m_xbc = sem("m_xbc")
        m_dt = sem("m_dt")
        m_de = sem("m_de")
        m_dec = sem("m_dec")
        m_ua = sem("m_ua")
        m_tp = sem("m_tp")
        m_g = sem("m_g")
        m_df = sem("m_df")
        m_bc = sem("m_bc")
        m_xn = sem("m_xn")
        m_lt = sem("m_lt")
        m_lc = sem("m_lc")
        m_tap = sem("m_tap")
        m_res = sem("m_res")
        m_yo = sem("m_yo")
        m_yb = sem("m_yb")
        m_yd = sem("m_yd")
        m_L = sem("m_L")
        m_E = sem("m_E")
        m_B = sem("m_B")
        m_gm = sem("m_gm")
        m_M = sem("m_M")
        m_xd = sem("m_xd")
        m_xdd = sem("m_xdd")
        m_y = sem("m_y")
        m_s = sem("m_s")
        m_st = sem("m_st")
        m_yg = sem("m_yg")
        m_sq = sem("m_sq")
        m_o = sem("m_o")
        m_ms = sem("m_ms")
        m_rs = sem("m_rs")
        m_fin = sem("m_fin")
        m_u = sem("m_u")
        x_view = t["L0_attn_a_x"].rearrange("b (t p) d -> p (b t) d", p=P)

        def past(eng, semaphore, value):
            if not isinstance(value, int) or value > 0:
                eng.wait_ge(semaphore, value)

        def groups(eng, body):
            body(0, 0)
            with eng.Fori(1, UNITS // 4 - 1) as g:
                body(g, 1)
            body(UNITS // 4 - 1, 2)

        def hs(f, e, i):
            return (4 * FT + (EXPERTS - 1) * FT) * f + (i if e == 0 else 4 * FT + (e - 1) * FT + i)

        projections = ([(0, b, j) for b in range(BATCH) for j in range(CONV)] +
                       [(h, b, CONV + j) for h in range(2) for b in range(BATCH) for j in range(XC)] +
                       [(1, b, j) for b in range(BATCH) for j in range(CONV)])
        early = len(projections) - BATCH * CONV
        conv_by = [i + 1 for i in range(BATCH * CONV)]

        def convolved(u):
            return u // (CONV * BATCH), u // CONV % BATCH, u % CONV

        def conv_out(u):
            h, b, c = convolved(u)
            return xbc[:, c, b * SEQ + h * HALF:b * SEQ + (h + 1) * HALF]

        def chunk_tile(i):
            return (i % 2) * BT + i // 2

        def tr_bank(k, i):
            return bank[(0 if k == 1 else 6) + i % 2]

        def acts(f):
            return (4 * FT + (EXPERTS - 1) * FT // 2) * f

        def part(n, k):
            b, side, h = (n - 1) // 4, (n - 1) // 2 % 2, (n - 1) % 2
            return parts16[:, side, k, b * SEQ + h * HALF:b * SEQ + (h + 1) * HALF]

        def ys(f, i):
            return (EXPERTS + 3) * f + i

        after_store, stored, dense_stored = [], [], []
        dense_total, sparse_total = [0, 0], [0, 0]
        for f in range(2):
            for i in range(EXPERTS + 3):
                r = ys(f, i) % 2
                if i < 4:
                    dense_total[r] += 16
                    after_store.append((s_yst[r], dense_total[r]))
                else:
                    sparse_total[r] += 16 * CT
                    after_store.append((s_ysc[r], sparse_total[r]))
                if i == 3:
                    dense_stored.append(list(dense_total))
            stored.append(list(sparse_total))

        block = ctx.enter_context(nc.Block())

        @block.sync
        def _(sp):
            sp.dma_start(x[:, 0:BT, :], x_view[:, 0:BT, :]).then_inc(s_xin[0], 16)
            for i, n in enumerate(("wq", "wk", "wv")):
                sp.dma_start(wqkv[:, i, :], t["L0_attn_a_" + n]).then_inc(s_w, 16)
            sp.dma_start(ident[:], t["ident"]).then_inc(s_w, 16)
            sp.dma_start(rot[:], t["rot"]).then_inc(s_w, 16)
            sp.dma_start(cosT[:], t["cos"]).then_inc(s_const, 16)
            sp.dma_start(sinT[:], t["sin"]).then_inc(s_const, 16)
            sp.dma_start(x[:, BT:TILES, :], x_view[:, BT:TILES, :]).then_inc(s_xin[1], 16)

            def later_loads():
                sp.dma_start(router[:], t["L0_ffn_router_w"]).then_inc(s_moew, 16)
                sp.dma_start(b1rows[:], t["L0_ffn_b1"].rearrange("e (f p) -> (e f) p", p=P)).then_inc(s_moew, 16)
                sp.dma_start(b2[:].rearrange("p e d -> p (e d)"),
                             t["L0_ffn_b2"].rearrange("e d -> (e d)").partition_broadcast(P)).then_inc(s_moew, 16)
                sp.dma_start(left[:], t["left"]).then_inc(s_moew, 16)
                sp.dma_start(own_row[:], t["own_row"]).then_inc(s_moew, 16)
                sp.dma_start(tri_tiny[:], t["tri_tiny"]).then_inc(s_moew, 16)
                sp.wait_ge(s_pool, 3)
                for f in range(2):
                    sp.dma_start(sorted_dram[f][0:SLOTS, 0:D].rearrange("(p m) d -> p m d", p=FILL),
                                 zeros[0:FILL].unsqueeze(1).to_broadcast([FILL, SLOTS // FILL, D])).then_inc(s_zero, 16)
                    sp.dma_start(sorted_dram[f][0:SLOTS, D:ROW], t["spare_row"], allow_slow_non_contiguous=True).then_inc(s_zero, 16)
                sp.dma_start(win_rows[:], t["L0_attn_b_in_proj_w"][0:6 * P, :].rearrange("(c p) d -> p c d", p=P)).then_inc(m_w, 16)
                sp.dma_start(wdt_rows[:], t["L0_attn_b_in_proj_w"][6 * P:PROJ, :]).then_inc(m_w, 16)
                sp.dma_start(wout_rows[:], t["L0_attn_b_out_proj_w"]).then_inc(m_w, 16)
                sp.dma_start(norm_w[:], t["L0_attn_b_norm_w"].unsqueeze(1)).then_inc(m_w, 16)
                sp.dma_start(gnorm_w[:], t["L0_attn_b_gnorm_w"].rearrange("(c p) -> p c", p=P),
                          allow_slow_non_contiguous=True).then_inc(m_w, 16)
                sp.dma_start(conv_w[:], t["L0_attn_b_conv_w"].rearrange("(c p) o k -> p c (o k)", p=P)).then_inc(m_w, 16)
                sp.dma_start(conv_b[:], t["L0_attn_b_conv_b"].rearrange("(c p) -> p c", p=P),
                          allow_slow_non_contiguous=True).then_inc(m_w, 16)
                for h in range(SHEADS):
                    sp.dma_start(d_col[(h % 2) * SW:(h % 2 + 1) * SW, h // 2:h // 2 + 1],
                                 t["L0_attn_b_D"][h:h + 1].partition_broadcast(SW)).then_inc(m_w, 16)
                sp.dma_start(dt_bias[:], t["L0_attn_b_dt_bias"].partition_broadcast(P)).then_inc(m_w, 16)
                sp.dma_start(a_log[:], t["L0_attn_b_A_log"].partition_broadcast(P)).then_inc(m_w, 16)
                sp.dma_start(after[:], t["after"]).then_inc(m_w, 16)
                sp.dma_start(upto[:], t["upto"]).then_inc(m_w, 16)

            def load(n, j):
                past(sp, s_sc, 16 * (n - 3))
                for a in range(PARTS):
                    src = qparts_dram[bass.ds(n, 1), a].to_broadcast([PARTS, HD, SEQ])
                    sp.dma_start(qa[a * PARTS * HD:(a + 1) * PARTS * HD, j % 4, :], src).then_inc(s_load[j % 4], 16)
                src = kparts_dram[bass.ds(n, 1)].rearrange("u c d n -> u (c d) n").to_broadcast([PARTS, PARTS * HD, SEQ])
                sp.dma_start(ka[0:SROWS, j % 4, :], src).then_inc(s_load[j % 4], 16)

            def max_rows_in(n, j):
                sp.wait_ge(s_mc, n + 1)
                for part in range(PARTS):
                    sp.dma_start(qa[KROWS + part:KROWS + part + 1, j % 4, :],
                                 maxrows[part * BT:(part + 1) * BT, j % 2, :]).then_inc(s_mrow, 16)

            for b in range(BATCH):
                for side, dst in enumerate((qparts_dram, kparts_dram)):
                    sp.wait_ge(s_parts, 2 * (2 * b + side) + 2)
                    for part in range(PARTS):
                        sp.dma_start(dst[b * HEADS:(b + 1) * HEADS, part, :, :],
                                     parts16[:, side, part, b * SEQ:(b + 1) * SEQ]).then_inc(s_pstore[b], 16)
                if b == 0:
                    sp.wait_ge(s_pstore[0], 16 * PARTS * 2)
                    sp.wait_ge(s_init, 2)
                    for n in range(3):
                        load(n, n)
            sp.wait_ge(s_pstore[1], 16 * PARTS * 2)
            max_rows_in(0, 0)

            def body(g, where):
                for j in range(4):
                    n = 4 * g + j
                    if where < 2 or j < 1:
                        load(n + 3, j + 3)
                    if where < 2 or j < 3:
                        max_rows_in(n + 1, j + 1)
                    if j == 1:
                        sp.dma_start(w1[:, bass.ds(g, 1), :], t["L0_ffn_W1"][bass.ds(g, 1)].rearrange("e d f -> d e f")).then_inc(s_ew, 16)
                    if j == 2:
                        sp.dma_start(w2[:, bass.ds(g, 1), :, :].rearrange("p e f d -> p (e f) d"),
                                     t["L0_ffn_W2"][bass.ds(g, 1)].rearrange("e (f p) d -> p (e f) d", p=P)).then_inc(s_ew, 16)
                if where == 0:
                    later_loads()

            groups(sp, body)

            def experts(f):
                for g in range(4):
                    yi = ys(f, g)
                    if g == 2:
                        sorted_rows(f)
                    sp.wait_ge(s_yc, yi + 1)
                    sp.dma_start(y_dram[f][g * HALF:(g + 1) * HALF, :].rearrange("(m p) d -> p m d", p=P),
                                 y_sb[:, yi % 2, :, :]).then_inc(s_yst[yi % 2], 16)
                for i in range(2):
                    sp.wait_ge(s_ysc[i], stored[f][i])
                for g in range(4):
                    sp.dma_start(gathered[:, 4 * g:4 * g + 4, :],
                                 y_dram[f][g * HALF:(g + 1) * HALF, :].rearrange("(m p) d -> p m d", p=P)).then_inc(s_ga[g], 16)

            def sorted_rows(f):
                sp.wait_ge(s_scat, 16 * TILES * (f + 1))
                for e in range(1, EXPERTS):
                    r0 = (e - 1) * CAP
                    sp.dma_start(sorted_x[:, e, 0:2, :], sorted_dram[f][r0:r0 + 2 * P, :].rearrange("(m p) d -> p m d", p=P)).then_inc(s_srt[e], 16)
                    sp.dma_start(sorted_x[0:CAP - 2 * P, e, 2, :], sorted_dram[f][r0 + 2 * P:r0 + CAP, :]).then_inc(s_srt[e], 16)

            if stage >= 1:
                experts(0)
            if stage >= 3:
                experts(1)
            if stage < 3:
                sp.wait_ge(s_ew, 32 * EXPERTS)
                sp.wait_ge(s_zero, 64)
                sp.wait_ge(s_moew, 16 * 6)
                sp.wait_ge(m_w, 16 * 15)
            sp.wait_ge(s_out, 16)

        @block.gpsimd
        def _(pool):
            pool.memset(neghalf[:], -0.5).then_inc(s_pool, 1)
            pool.memset(ones[:], 1.0).then_inc(s_pool, 1)
            pool.memset(zeros[:], 0.0).then_inc(s_pool, 1)
            pool.wait_ge(s_pool, 3)

            def rsqrt(k, src, batches=range(BATCH)):
                for b in batches:
                    pool.wait_ge(s_ln, 2 * k + b + 1)
                    tl = slice(b * BT, (b + 1) * BT)
                    pool.tensor_tensor(src[:, tl], src[:, tl], neghalf[:, tl], ALU.pow).then_inc(s_rstd, 1)

            rsqrt(0, rstd)
            pool.memset(qa[:].bitcast(F32), 0.0).then_inc(s_init, 1)
            pool.memset(routerT[:], 0.0)
            pool.memset(wdtT[:], 0.0)
            pool.memset(vstage[:], 0.0).then_inc(s_pool, 1)
            pool.wait_ge(s_pool, 4)
            pool.memset(vstage[:, 0, :, HD:UCOL], 1.0)
            pool.memset(vstage[:, 1, :, UCOL + HD:2 * UCOL], 1.0).then_inc(s_pool, 1)

            for n in range(1, 8 + 2):
                if n <= 8:
                    pool.wait_ge(s_projc, n)
                    pool.tensor_tensor(rope_a[:, n % RING, :], rope_a[:, n % RING, :], rope_b[:, n % RING, :], ALU.add).then_inc(s_rs, 1)
                if n >= 2:
                    pool.wait_ge(s_p1, n - 1)
                    pool.tensor_tensor(rope_b[:, (n - 1) % RING, :], rope_a[:, (n - 1) % RING, :], part(n - 1, 0),
                                       ALU.subtract).then_inc(s_r1, 1)

            pool.wait_ge(s_valc, 2 * TILES // 8)

            def max_parts(n, j):
                pool.wait_ge(s_mx, BT * (n + 1))
                past(pool, s_mt, n)
                c = 4 * n
                pool.tensor_tensor(maxparts[:, 0, :], negmax[:, j % 2, :], zeros[:, 0:BT], ALU.add).then_inc(s_pl, 1)
                pool.wait_ge(s_pl, c + 1)
                pool.tensor_tensor(maxrest[:, 0, :], negmax[:, j % 2, :], maxparts[:, 0, :], ALU.subtract).then_inc(s_pl, 1)
                pool.wait_ge(s_pl, c + 2)
                pool.tensor_tensor(maxparts[:, 1, :], maxrest[:, 0, :], zeros[:, 0:BT], ALU.add).then_inc(s_pl, 1)
                pool.wait_ge(s_pl, c + 3)
                pool.tensor_tensor(maxrest[:, 1, :], maxrest[:, 0, :], maxparts[:, 1, :], ALU.subtract).then_inc(s_pl, 1)
                pool.wait_ge(s_pl, c + 4)
                pool.tensor_tensor(maxparts[:, 2, :], maxrest[:, 1, :], zeros[:, 0:BT], ALU.add).then_inc(s_mp, 1)

            def weigh(p):
                pool.wait_ge(s_od, p + 1)
                pool.tensor_tensor(att[:, bass.ds(2 * p, 2), :, :],
                                   osum[:].rearrange("p t (u c) -> p u t c", u=2)[:, :, :, 0:HD],
                                   orec[:].rearrange("p t u -> p u t").unsqueeze(3).to_broadcast([P, 2, BT, HD]),
                                   ALU.mult).then_inc(s_at, 1)

            pool.wait_ge(s_init, 2)
            pool.wait_ge(s_r1, 8)
            pool.memset(ka[KROWS:KROWS + PARTS, :, :], 1.0).then_inc(s_ones, 1)
            pool.wait_ge(s_ones, 1)
            max_parts(0, 0)
            max_parts(1, 1)

            def body(g, where):
                for j in range(4):
                    n = 4 * g + j
                    past(pool, s_pv, 4 * (4 * g + j - 1))
                    pool.tensor_tensor(vstage[:, j % 2, :, (j % 2) * UCOL:(j % 2) * UCOL + HD],
                                       values[:, bass.ds(4 * g + j, 1), :, :].rearrange("p u t d -> p (u t) d"),
                                       zeros[:, 0:BT * HD].rearrange("p (t d) -> p t d", t=BT), ALU.add).then_inc(s_vst, 1)
                    if j % 2 == 0 and (where > 0 or j > 0):
                        weigh(2 * g + j // 2 - 1)
                    if where < 2 or j < 2:
                        max_parts(n + 2, j)
                    if where == 2 and j == 2 and stage >= 1:
                        rsqrt(1, rstd, [0])

            groups(pool, body)
            weigh(PAIRS - 1)

            def experts(f, k):
                rsqrt(k, rstd, [0, 1] if f else [1])
                pool.wait_ge(s_zero, 64)
                for i in range(TILES):
                    if i % 4 == 0:
                        pool.wait_ge(s_slot, 4 * f + i // 4 + 1)
                    pool.indirect_dma_start(sorted_dram[f][:, :], bass.IndirectOffsetOnAxis(ap=slot[:, i:i + 1], axis=0),
                                            xn[:, i, :], None).then_inc(s_scat, 16)
                for i in range(2):
                    pool.wait_ge(s_yst[i], dense_stored[f][i])
                for e in range(1, EXPERTS):
                    yi = ys(f, 3 + e)
                    pool.wait_ge(s_yc, yi + 1)
                    pool.wait_ge(s_dest, (EXPERTS - 1) * f + e)
                    for m in range(CT):
                        n = min(P, CAP - m * P)
                        pool.indirect_dma_start(y_dram[f][:, :], bass.IndirectOffsetOnAxis(ap=dest[0:n, e, m:m + 1], axis=0),
                                                y_sb[0:n, yi % 2, m, :], None).then_inc(s_ysc[yi % 2], 16)

            def state_space(k):
                pool.memset(before_conv[:, :, :, 0:TAPS - 1], 0.0).then_inc(m_pad, 1)
                rsqrt(k, rstd)
                rsqrt(k + 1, rms)
                pool.wait_ge(m_xn, BATCH)
                pool.tensor_tensor(x[:], x[:], xn[:, :, 0:D], ALU.add).then_inc(m_res, 1)

                def segments(i):
                    T = chunk_tile(i)
                    if i == 0:
                        pool.wait_ge(m_dec, 1)
                    past(pool, m_df, i - 1)
                    pool.tensor_tensor(seg[:, i % 2, :, :], after[:].unsqueeze(1).to_broadcast([P, SHEADS, P]),
                                       log_decay[:, T, :].unsqueeze(2).to_broadcast([P, SHEADS, P]), ALU.mult).then_inc(m_ua, 1)

                thin = [P, SHEADS, SW]
                segments(0)
                for i in range(TILES + 3):
                    if i + 1 < TILES:
                        segments(i + 1)
                    if i < TILES:
                        T, r, b, c = chunk_tile(i), i % 2, i % 2, i // 2
                        pool.wait_ge(m_L, i + 1)
                        pool.wait_ge(m_xd, i + 1)
                        past(pool, m_s, i - 1)
                        pool.tensor_tensor(xdd[:, r, :, :], xd[:, r, :, :], decay[:, r, :, LAST:P].to_broadcast(thin),
                                           ALU.mult).then_inc(m_xdd, 1)
                        if c > 0:
                            pool.wait_ge(m_E, 1)
                            pool.wait_ge(m_st, i - 1)
                            pool.tensor_tensor(st_tmp[:, r, :, :], state[:, b, c % 2, :, :],
                                               grown[:, 1, T, :].unsqueeze(2).to_broadcast(thin), ALU.mult).then_inc(m_yd, 1)
                    if i >= 3:
                        T = chunk_tile(i - 3)
                        pool.wait_ge(m_ms, i - 2)
                        pool.tensor_tensor(ysum[:, T:T + 1], ysum[:, T:T + 1], neghalf[:, 0:1], ALU.pow).then_inc(m_rs, 1)

            if stage >= 1:
                experts(0, 1)
            if stage >= 2:
                state_space(2)
            if stage >= 3:
                experts(1, 4)

        @block.vector
        def _(dve):
            steps = [0]

            def link(ins):
                steps[0] += 1
                ins.then_inc(s_dve, 1)
                dve.wait_ge(s_dve, steps[0])

            def layernorm(b, k):
                for i in range(b * BT, (b + 1) * BT):
                    ins = dve.bn_stats(stats[:, i, :], x[:, i, :])
                link(ins)
                for i in range(b * BT, (b + 1) * BT):
                    ins = dve.bn_aggr(meanvar[:, i, :], stats[:, i, :])
                link(ins)
                tl = slice(b * BT, (b + 1) * BT)
                dve.tensor_scalar(rstd[:, tl], meanvar[:, tl, 1], EPS, None, ALU.add).then_inc(s_ln, 1)

            def normalise(b, k):
                dve.wait_ge(s_rstd, 2 * k + b + 1)
                for i in range(b * BT, (b + 1) * BT):
                    ins = dve.tensor_scalar(xn[:, i, 0:D], x[:, i, :], meanvar[:, i, 0:1], rstd[:, i:i + 1],
                                            ALU.subtract, ALU.mult)
                ins.then_inc(s_xn, 1)

            dve.wait_ge(s_w, 80)
            dve.tensor_copy(ident16[:], ident[:]).then_inc(s_id16, 1)
            for b in range(BATCH):
                dve.wait_ge(s_xin[b], 16)
                layernorm(b, 0)
                normalise(b, 0)
            def rope_products(n):
                pos = slice((n - 1) % 2 * HALF, ((n - 1) % 2 + 1) * HALF)
                dve.wait_ge(s_proj, n)
                past(dve, s_parts, n - RING)
                dve.tensor_tensor(rope_a[:, n % RING, :], bank[(2 * n) % 4], cosT[:, pos], ALU.mult)
                dve.tensor_tensor(rope_b[:, n % RING, :], bank[(2 * n + 1) % 4], sinT[:, pos], ALU.mult).then_inc(s_projc, 1)

            def second_rest(n):
                dve.wait_ge(s_p2, n)
                dve.tensor_tensor(rope_a[:, n % RING, :], rope_b[:, n % RING, :], part(n, 1), ALU.subtract).then_inc(s_r2, 1)

            dve.wait_ge(s_const, 32)
            for n in range(1, 8 + 3):
                if n <= 8:
                    rope_products(n)
                if n >= 3:
                    second_rest(n - 2)
                if n == 3:
                    dve.memset(ka[:].bitcast(F32), 0.0).then_inc(s_init, 1)

            def maxima(n, j, tiles):
                past(dve, s_pl, 4 * (n - 1) - 2)
                for i in tiles:
                    dve.wait_ge(s_ms, BT * n + i + 1)
                    dve.tensor_reduce(negmax[:, j % 2, i:i + 1], mbank[:, i % 2, :], AX.X, ALU.max,
                                      negate=True).then_inc(s_mx, 1)

            def finish(p):
                dve.wait_ge(s_ot, p + 1)
                past(dve, s_at, p)
                for qh in range(2):
                    src = bank[7].rearrange("p (b e q c) -> p b q c e", b=4, e=2, q=2)[:, :, qh, 0:2 * UCOL, :]
                    dve.tensor_reduce(osum[:, qh * 4:(qh + 1) * 4, :], src, AX.X, ALU.add).then_inc(s_oa, 1)
                dve.wait_ge(s_oa, 2 * p + 2)
                dve.reciprocal(orec[:], osum[:].rearrange("p t (u c) -> p t u c", u=2)[:, :, :, HD]).then_inc(s_od, 1)

            def residual(b):
                tl = slice(b * BT, (b + 1) * BT)
                dve.wait_ge(s_at, HEADS // 2 * (b + 1))
                link(dve.tensor_tensor(x[:, tl, :].rearrange("p t (h d) -> p t h d", h=HEADS),
                                       x[:, tl, :].rearrange("p t (h d) -> p t h d", h=HEADS),
                                       att[:, b * HEADS:(b + 1) * HEADS, :, :].rearrange("p h t d -> p t h d"), ALU.add))

            maxima(0, 0, range(BT))
            maxima(1, 1, range(BT))

            def body(g, where):
                for j in range(4):
                    n = 4 * g + j
                    ahead = where < 2 or j < 2
                    if ahead:
                        maxima(n + 2, j, range(FINISH))
                    if j % 2 == 0 and (where > 0 or j > 0):
                        finish(2 * g + j // 2 - 1)
                    if where == 2 and j == 0:
                        residual(0)
                    if where == 2 and j == 1 and stage >= 1:
                        layernorm(0, 1)
                    if where == 2 and j == 2 and stage >= 1:
                        normalise(0, 1)
                    if ahead:
                        maxima(n + 2, j, range(FINISH, BT))

            groups(dve, body)
            finish(PAIRS - 1)
            residual(1)

            def experts(f, k):
                if f == 0:
                    layernorm(1, k)
                    normalise(1, k)
                else:
                    for b in range(BATCH):
                        layernorm(b, k)
                    for b in range(BATCH):
                        normalise(b, k)
                top, total_e, prob, left_of, rank, chosen, place, base, elsewhere = (r8[:, i, :] for i in range(9))
                wide = [P, TILES, EXPERTS]
                dve.wait_ge(s_rt, f + 1)
                logits = bank[4].rearrange("p (c q e) -> p q c e", c=4, q=4)[:, :, :, 0:EXPERTS]
                link(dve.tensor_reduce(top.rearrange("p (q c) -> p q c", q=4), logits, AX.X, ALU.max))
                link_to(dve.tensor_tensor(z_log[:].rearrange("p (q c) e -> p q c e", q=4), logits,
                                          top.rearrange("p (q c) -> p q c", q=4).unsqueeze(3).to_broadcast([P, 4, 4, EXPERTS]),
                                          ALU.subtract), s_zl, f + 1)
                if f == 0:
                    dve.wait_ge(s_moew, 16 * 6)
                leftb = left[:].unsqueeze(1).to_broadcast(wide)
                link(dve.scalar_tensor_tensor(w_log[:], z_log[:], 0.0, leftb, ALU.is_equal, ALU.mult))
                dve.wait_ge(s_el, f + 1)
                dve.tensor_reduce(left_of, w_log[:], AX.X, ALU.max)
                link(dve.tensor_reduce(total_e, e_log[:], AX.X, ALU.add))
                link(dve.reciprocal(prob, total_e))
                for c in range(4):
                    dve.tensor_tensor(diag[:, 4 * c:4 * c + 4, :], ident[:].unsqueeze(1).to_broadcast([P, 4, P]),
                                      prob[:, 4 * c:4 * c + 4].unsqueeze(2).to_broadcast([P, 4, P]), ALU.mult).then_inc(s_dg, 1)
                dve.tensor_tensor(onehot[:], leftb, left_of.unsqueeze(2).to_broadcast(wide), ALU.is_equal).then_inc(s_oh, 1)
                dve.tensor_scalar(elsewhere, left_of, float(EXPERTS), None, ALU.is_lt)
                link(dve.scalar_tensor_tensor(base, left_of, -float(CAP), own_row[:], ALU.mult, ALU.subtract))
                link(dve.tensor_scalar(base, base, float(SLOTS), None, ALU.add))
                if f == 0:
                    dve.tensor_scalar(xn[:, :, D], own_row[:], -float(SLOTS), None, ALU.add)

                def slots(g):
                    tl = slice(4 * g, 4 * g + 4)
                    dve.wait_ge(s_rk, STEPS * f + TILES * (g + 1))
                    link(dve.tensor_tensor(w_log[:, tl, :], bank[g][:, 0:4 * EXPERTS].rearrange("p (t e) -> p t e", t=4),
                                           onehot[:, tl, :], ALU.mult))
                    link(dve.tensor_reduce(rank[:, tl], w_log[:, tl, :], AX.X, ALU.add))
                    dve.scalar_tensor_tensor(chosen[:, tl], rank[:, tl], float(CAP), elsewhere[:, tl], ALU.is_lt, ALU.mult)
                    link(dve.tensor_tensor(place[:, tl], rank[:, tl], base[:, tl], ALU.add))
                    link(dve.tensor_tensor(place[:, tl], place[:, tl], chosen[:, tl], ALU.mult))
                    dve.tensor_tensor(slot[:, tl], place[:, tl], own_row[:, tl], ALU.add).then_inc(s_slot, 1)

                for n in range(STEPS):
                    g, j = n // TILES, n % TILES
                    if j == 0:
                        dve.wait_ge(s_pwc, 4 * f + g + 1)
                    past(dve, s_rk, STEPS * f + max(0, n - RANK_RING + 1))
                    pj = prob[:, j:j + 1]
                    columns = prow[:, g * HALF:(g + 1) * HALF]
                    if j // 4 == g:
                        own = (3 - j % 4) * P
                        ins = dve.scalar_tensor_tensor(before[:, n % RANK_RING, :], columns, pj, tri_tiny[:, own:own + HALF], ALU.subtract, ALU.is_lt)
                    else:
                        ins = dve.tensor_scalar(before[:, n % RANK_RING, :], columns, pj, None, ALU.is_lt if g < j // 4 else ALU.is_le)
                    ins.then_inc(s_bf, 1)
                    if g > 0 and j == 3:
                        slots(g - 1)
                    if n in OUT_STEPS:
                        y_out(f, OUT_STEPS.index(n))
                slots(3)
                y_out(f, 2)
                y_out(f, 3)
                for e in range(1, EXPERTS):
                    sorted_out(f, e)
                    if e > 1:
                        for i in (1, 3):
                            hidden_out(f, e - 1, i)
                    if e > 2:
                        y_out(f, 3 + e - 2)
                for i in (1, 3):
                    hidden_out(f, EXPERTS - 1, i)
                y_out(f, 3 + EXPERTS - 2)
                y_out(f, 3 + EXPERTS - 1)

            def sorted_out(f, e):
                dve.wait_ge(s_st, (EXPERTS - 1) * f + e)
                dve.tensor_copy(sortedT[:, (e - 1) * CAP:e * CAP], bank[(4, 7)[e % 2]][:, 0:CAP]).then_inc(s_stc, 1)
                dve.wait_ge(s_srt[e], 32 * (f + 1))
                dve.tensor_copy(dest[:, e, 0:2], sorted_x[:, e, 0:2, D])
                dve.tensor_copy(dest[0:CAP - 2 * P, e, 2:3], sorted_x[0:CAP - 2 * P, e, 2, D:ROW]).then_inc(s_dest, 1)

            def add_experts(f, groups_of_tiles):
                for g in groups_of_tiles:
                    dve.wait_ge(s_ga[g], 16 * (f + 1))
                    ins = dve.tensor_tensor(x[:, 4 * g:4 * g + 4, :], x[:, 4 * g:4 * g + 4, :],
                                            gathered[:, 4 * g:4 * g + 4, :], ALU.add)
                link(ins)

            def link_to(ins, semaphore, value):
                ins.then_inc(semaphore, 1)
                dve.wait_ge(semaphore, value)

            def hidden_out(f, e, i):
                h = hs(f, e, i)
                dve.wait_ge(s_h, h + 1)
                dve.wait_ge(s_y, ys(f, 3) if e == 1 else ys(f, 3 + e - 2) + 1)
                dve.tensor_scalar(hidden[:, e % 2, i, 0:CAP], bank[i][:, 0:CAP], b1T[:, e * FT + i:e * FT + i + 1], 0.0,
                                  ALU.add, ALU.max).then_inc(s_hv, 1)

            def y_out(f, i):
                yi = ys(f, i)
                dve.wait_ge(s_y, yi + 1)
                if yi >= 2:
                    dve.wait_ge(*after_store[yi - 2])
                if i < 4:
                    dve.tensor_tensor(y_sb[:, yi % 2, :, :], bank[6].rearrange("p (m d) -> p m d", m=4),
                                      b2[:, 0, :].unsqueeze(1).to_broadcast([P, 4, D]), ALU.add).then_inc(s_yc, 1)
                else:
                    e = i - 3
                    src = bank[5 + e % 2].rearrange("p (m d) -> p m d", m=4)
                    dve.tensor_tensor(y_sb[:, yi % 2, 0:2, :], src[:, 0:2, :],
                                      b2[:, e, :].unsqueeze(1).to_broadcast([P, 2, D]), ALU.add)
                    dve.tensor_tensor(y_sb[0:CAP - 2 * P, yi % 2, 2, :], src[0:CAP - 2 * P, 2, :],
                                      b2[0:CAP - 2 * P, e, :], ALU.add).then_inc(s_yc, 1)

            def softplus():
                v, e, z, z2, p, q = (sp_tmp[:, i, :] for i in range(6))
                by_head = "p (t h) -> p t h"
                dve.wait_ge(m_dt, 1)
                link(dve.tensor_tensor(v.rearrange("p (q c h) -> p q c h", q=4, c=4),
                                       bank[4].rearrange("p (c q h) -> p q c h", c=4, q=4)[:, :, :, 0:SHEADS],
                                       dt_bias[:].unsqueeze(1).unsqueeze(1).to_broadcast([P, 4, 4, SHEADS]), ALU.add))
                dve.scalar_tensor_tensor(q, v, -1.0, v, ALU.mult, ALU.min).then_inc(m_dt, 1)
                dve.wait_ge(m_de, 1)
                link(dve.tensor_scalar(z2, e, 2.0, None, ALU.add))
                link(dve.reciprocal(p, z2))
                link(dve.tensor_tensor(z, e, p, ALU.mult))
                link(dve.tensor_tensor(z2, z, z, ALU.mult))
                link(dve.tensor_scalar(p, z2, 1.0 / 17, None, ALU.mult))
                for n in range(15, 1, -2):
                    link(dve.scalar_tensor_tensor(p, p, 1.0 / n, z2, ALU.add, ALU.mult))
                link(dve.scalar_tensor_tensor(q, p, 1.0, z, ALU.add, ALU.mult))
                link(dve.tensor_scalar(q, q, 2.0, None, ALU.mult))
                link(dve.scalar_tensor_tensor(dt[:].rearrange("p t h -> p (t h)"), v, 0.0, q, ALU.max, ALU.add))
                dve.tensor_tensor(log_decay[:], dt[:], neg_a[:].unsqueeze(1).to_broadcast([P, TILES, SHEADS]),
                                  ALU.mult).then_inc(m_dec, 1)

            def state_space(k):
                for b in range(BATCH):
                    add_experts(0, [2 * b, 2 * b + 1])
                    layernorm(b, k)
                for b in range(BATCH):
                    tl = slice(b * BT, (b + 1) * BT)
                    dve.wait_ge(s_rstd, 2 * k + b + 1)
                    link(dve.tensor_tensor(rms[:, tl], meanvar[:, tl, 1], rstd[:, tl], ALU.mult))
                    link(dve.tensor_tensor(rms[:, tl], rms[:, tl], rstd[:, tl], ALU.mult))
                    dve.tensor_scalar(rms[:, tl], rms[:, tl], EPS, None, ALU.add).then_inc(s_ln, 1)
                for b in range(BATCH):
                    for i in range(b * BT, (b + 1) * BT):
                        ins = dve.tensor_scalar(xn[:, i, 0:D], x[:, i, :], meanvar[:, i, 0:1], rstd[:, i:i + 1],
                                                ALU.subtract, ALU.mult)
                    ins.then_inc(m_xn, 1)
                dve.wait_ge(s_nega, 1)
                link(dve.tensor_scalar(neg_a[:], neg_a[:], -1.0, None, ALU.mult))
                softplus()

                def convolve(u):
                    h, b, c = convolved(u)
                    dve.wait_ge(m_tap, u + 1)
                    for w in range(1, TAPS):
                        ins = dve.scalar_tensor_tensor(conv_out(u), before_conv[:, c, b, h * HALF + w:h * HALF + w + HALF],
                                                       conv_w[:, c, w:w + 1], conv_out(u), ALU.mult, ALU.add)
                        if w < TAPS - 1:
                            link(ins)
                    ins.then_inc(m_conv, 1)

                for u in range(CONV * BATCH):
                    convolve(u)

                def chunk_a(i):
                    T, r = chunk_tile(i), i % 2
                    wide = [P, SHEADS, P]
                    thin = [P, SHEADS, SW]
                    dve.wait_ge(m_g, i + 1)
                    dve.tensor_tensor(cb[:, r, :], bank[1][:, 0:P], upto[:], ALU.mult).then_inc(m_gm, 1)
                    dve.wait_ge(m_B, i + 1)
                    past(dve, m_y, i - 1)
                    past(dve, m_xdd, i - 1)
                    dve.tensor_tensor(xd[:, r, :, :], bank[0][:, 0:INNER].rearrange("p (h w) -> p h w", h=SHEADS),
                                      dt[:, T, :].unsqueeze(2).to_broadcast(thin), ALU.mult).then_inc(m_xd, 1)
                    dve.wait_ge(m_L, i + 1)
                    dve.wait_ge(m_gm, i + 1)
                    dve.tensor_tensor(mix[:, r, :, :], decay[:, r, :, :], cb[:, r, :].unsqueeze(1).to_broadcast(wide),
                                      ALU.mult).then_inc(m_M, 1)

                def state_output(i):
                    T, r = chunk_tile(i), i % 2
                    if i // 2 > 0:
                        dve.wait_ge(m_E, 1)
                        dve.wait_ge(m_yo, i - 1)
                        dve.tensor_tensor(y_before[:, r, :, :], bank[1][:, P:P + INNER].rearrange("p (h w) -> p h w", h=SHEADS),
                                          grown[:, 0, T, :].unsqueeze(2).to_broadcast([P, SHEADS, SW]), ALU.mult).then_inc(m_yb, 1)

                def chunk_b(i):
                    T, r, b, c = chunk_tile(i), i % 2, i % 2, i // 2
                    new = bank[5][:, 0:INNER].rearrange("p (h w) -> p h w", h=SHEADS)
                    dve.wait_ge(m_s, i + 1)
                    if c > 0:
                        dve.wait_ge(m_yd, i - 1)
                        dve.tensor_tensor(state[:, b, (c + 1) % 2, :, :], new, st_tmp[:, r, :, :], ALU.add).then_inc(m_st, 1)
                    else:
                        dve.tensor_copy(state[:, b, (c + 1) % 2, :, :], new).then_inc(m_st, 1)
                    dve.wait_ge(m_y, i + 1)
                    dve.wait_ge(m_xbc, CONV * (i % 2 + 1) if c < BT // 2 else CONV * (BATCH + i % 2 + 1))
                    past(dve, m_yg, i)
                    for ct in range(XC):
                        ins = dve.scalar_tensor_tensor(y_dx[:, ct, :], xbc[:, ct, T * P:(T + 1) * P], d_col[:, ct:ct + 1],
                                                       bank[4][:, ct * P:(ct + 1) * P], ALU.mult, ALU.add)
                    ins.then_inc(m_u, 1)
                    dve.wait_ge(m_u, i + 1)
                    past(dve, m_o, i - 2)
                    past(dve, m_sq, i - 2)
                    dve.tensor_tensor(yg[:, i % 3, :, :], y_dx[:], gate[:, :, T * P:(T + 1) * P], ALU.mult).then_inc(m_yg, 1)

                def chunk_c(i):
                    T = chunk_tile(i)
                    dve.wait_ge(m_o, i + 1)
                    dve.tensor_scalar(ysum[:, T:T + 1], bank[6 + i % 2][:, P:P + 1], 1.0 / INNER, EPS, ALU.mult,
                                      ALU.add).then_inc(m_ms, 1)

                def chunk_d(i):
                    T = chunk_tile(i)
                    dve.wait_ge(m_rs, i + 1)
                    if i == 0:
                        dve.wait_ge(m_res, 1)
                    dve.scalar_tensor_tensor(x[:, T, :], bank[6 + i % 2][:, 0:P], ysum[:, T:T + 1], x[:, T, :],
                                             ALU.mult, ALU.add).then_inc(m_fin, 1)

                for i in range(TILES + 4):
                    if 1 <= i <= TILES:
                        state_output(i - 1)
                    if i < TILES:
                        chunk_a(i)
                    if i < CONV * BATCH:
                        for u in range(conv_by[i - 1] if i else 0, conv_by[i]):
                            convolve(CONV * BATCH + u)
                    if 1 <= i <= TILES:
                        chunk_b(i - 1)
                    if i >= 4:
                        chunk_d(i - 4)
                    if 3 <= i < TILES + 3:
                        chunk_c(i - 3)
                dve.wait_ge(m_fin, TILES)

            if stage >= 1:
                experts(0, 1)
            if stage >= 2:
                state_space(2)
            if stage >= 3:
                experts(1, 4)
            if stage == 1 or stage >= 3:
                add_experts(0 if stage == 1 else 1, range(4))
            dve.sem_inc(s_x, 1)

        @block.scalar
        def _(act):
            act.wait_ge(s_wt, 1)
            act.activation(wT[:, 0:4, :], bank[4].rearrange("p (a b) -> p a b", a=4), ACT.Copy).then_inc(s_wtc, 1)
            act.wait_ge(s_wt, 2)
            act.activation(wT[:, 4, :], bank[5][:, 0:P], ACT.Copy).then_inc(s_wtc, 1)

            def transposed(k, groups_of_tiles=range(4)):
                for i in [4 * k + g for g in groups_of_tiles]:
                    act.wait_ge(s_tr, i + 1)
                    act.activation(xnT[:, (i % 4) * HALF:(i % 4 + 1) * HALF], tr_bank(k, i), ACT.Copy).then_inc(s_trc, 1)

            transposed(0, [0, 1])
            for n in range(1, 8 + 3):
                if n == 3:
                    transposed(0, [2, 3])
                if 5 <= n < 5 + TILES // 4:
                    i = n - 5
                    act.wait_ge(s_val, i + 1)
                    b, t0 = i // 2, 4 * (i % 2)
                    act.activation(values[:, b * HEADS:(b + 1) * HEADS, t0:t0 + 4, :].rearrange("p h t d -> p t h d"),
                                   bank[4 + i % 2].rearrange("p (t h d) -> p t h d", t=4, h=HEADS), ACT.Copy).then_inc(s_valc, 1)
                if n <= 8:
                    act.wait_ge(s_rs, n)
                    act.activation(part(n, 0), rope_a[:, n % RING, :], ACT.Copy).then_inc(s_p1, 1)
                if 2 <= n <= 9:
                    act.wait_ge(s_r1, n - 1)
                    act.activation(part(n - 1, 1), rope_b[:, (n - 1) % RING, :], ACT.Copy).then_inc(s_p2, 1)
                if n >= 3:
                    act.wait_ge(s_r2, n - 2)
                    act.activation(part(n - 2, 2), rope_a[:, (n - 2) % RING, :], ACT.Copy).then_inc(s_parts, 1)
            def body(g, where):
                for j in range(4):
                    n = 4 * g + j
                    for i in range(16):
                        act.wait_ge(s_sc, 16 * n + i + 1)
                        if i % 4 == 0:
                            past(act, s_pv, 4 * n + i // 4 - 1)
                        act.activation(probs[:, (i // 2) % 4, (i % 2) * HALF:(i % 2 + 1) * HALF], bank[4 + i % 2],
                                       ACT.Exp, scale=ATT_SCALE).then_inc(s_pr, 1)
                        if i == 2 and j % 2 == 0 and (where > 0 or j > 0):
                            o_copy(2 * g + j // 2 - 1)
                        if i == ROWS_OUT and (where < 2 or j < 3):
                            rows_out(n + 1, j + 1)

            def rows_out(n, j):
                act.wait_ge(s_mt, n + 1)
                past(act, s_mrow, 16 * PARTS * (n - 1))
                act.activation(maxrows[:, j % 2, :], mtrans, ACT.Copy).then_inc(s_mc, 1)

            rows_out(0, 0)

            def o_copy(p):
                act.wait_ge(s_pv, 8 * (p + 1))
                past(act, s_ot, p)
                act.activation(o_sb[:], bank[6], ACT.Copy).then_inc(s_oc, 1)

            groups(act, body)
            o_copy(PAIRS - 1)

            def relu(f, e, i, cols, src, dst):
                h = hs(f, e, i)
                act.wait_ge(s_h, h + 1)
                act.activation(dst, src, ACT.Relu, bias=b1T[:, e * FT + (i % FT):e * FT + (i % FT) + 1]).then_inc(s_ha, 1)

            def experts(f, k):
                if f == 0:
                    act.wait_ge(s_wt, 3)
                    act.activation(routerT[:, 0:EXPERTS], bank[5][:, 0:EXPERTS], ACT.Copy)
                    act.activation(b1T[:], bank[5][:, P:P + EXPERTS * FT], ACT.Copy).then_inc(s_wtc, 1)
                transposed(k)
                act.wait_ge(s_lt, f + 1)
                act.activation(prow[:, 0:HALF], bank[4], ACT.Copy).then_inc(s_lc, 1)
                act.wait_ge(s_zl, f + 1)
                act.activation(e_log[:], z_log[:], ACT.Exp).then_inc(s_el, 1)
                for i in range(16):
                    g = i // FT
                    if i == EARLY:
                        for c in range(4):
                            act.wait_ge(s_pw, 4 * f + c + 1)
                            act.activation(prow[:, c * HALF:(c + 1) * HALF], bank[c], ACT.Copy).then_inc(s_pwc, 1)
                    if g >= 2 and i % FT == 0:
                        act.wait_ge(s_y, ys(f, g - 2) + 1)
                    relu(f, 0, i, HALF, bank[(5, 7)[i % 2]], hidden[:, g % 2, i % FT, :])
                for e in range(1, EXPERTS):
                    for i in (0, 2):
                        if e == 1:
                            act.wait_ge(s_y, ys(f, 3))
                        else:
                            act.wait_ge(s_y, ys(f, 3 + e - 2) + 1)
                        relu(f, e, i, CAP, bank[i][:, 0:CAP], hidden[:, e % 2, i, 0:CAP])

            def state_space(kt):
                act.wait_ge(m_w, 16 * 15)
                act.activation(neg_a[:], a_log[:], ACT.Exp).then_inc(s_nega, 1)
                for j in range(3):
                    act.wait_ge(m_wt, j + 1)
                    if j == 0:
                        act.activation(winT[:, 0:4 * P], bank[0], ACT.Copy, scale=norm_w[:, 0:1]).then_inc(m_wc, 1)
                    elif j == 1:
                        act.activation(winT[:, 4 * P:6 * P], bank[1][:, 0:2 * P], ACT.Copy, scale=norm_w[:, 0:1]).then_inc(m_wc, 1)
                        act.activation(wdtT[:, 0:SHEADS], bank[1][:, 2 * P:2 * P + SHEADS], ACT.Copy, scale=norm_w[:, 0:1]).then_inc(m_wc, 1)
                    else:
                        for c in range(XC):
                            act.activation(woutT[:, c, :], bank[2][:, c * P:(c + 1) * P], ACT.Copy,
                                           scale=gnorm_w[:, c:c + 1]).then_inc(m_wc, 1)
                for b in range(BATCH):
                    act.wait_ge(m_xn, b + 1)
                    act.wait_ge(s_rstd, 2 * (kt + 1) + b + 1)
                    for i in range(b * BT, (b + 1) * BT):
                        ins = act.activation(un[:, i, :], xn[:, i, 0:D], ACT.Copy, scale=rms[:, i:i + 1])
                    ins.then_inc(s_xn, 1)
                transposed(kt)
                act.wait_ge(m_lt, 1)
                act.activation(dtT[:], bank[4], ACT.Copy).then_inc(m_lc, 1)
                act.wait_ge(m_dt, 2)
                act.activation(sp_tmp[:, 1, :], sp_tmp[:, 5, :], ACT.Exp).then_inc(m_de, 1)
                act.wait_ge(m_pad, 1)

                def projected(n):
                    h, b, j = projections[n]
                    act.wait_ge(m_zx, n + 1)
                    src = bank[n % 4] if n < early else bank[3]
                    if j < CONV:
                        act.activation(before_conv[:, j, b, TAPS - 1 + h * HALF:TAPS - 1 + (h + 1) * HALF], src, ACT.Copy).then_inc(m_zc, 1)
                    else:
                        act.activation(gate[:, j - CONV, b * SEQ + h * HALF:b * SEQ + (h + 1) * HALF], src,
                                       ACT.Silu).then_inc(m_zc, 1)

                def first_tap(u):
                    h, b, c = convolved(u)
                    act.wait_ge(m_zc, early * h + u % (CONV * BATCH) + 1)
                    act.activation(conv_out(u), before_conv[:, c, b, h * HALF:h * HALF + HALF], ACT.Copy,
                                   scale=conv_w[:, c, 0:1]).then_inc(m_tap, 1)

                def activate(u):
                    c = convolved(u)[2]
                    act.wait_ge(m_conv, u + 1)
                    act.activation(conv_out(u), conv_out(u), ACT.Silu, bias=conv_b[:, c:c + 1]).then_inc(m_xbc, 1)

                for n in range(early):
                    projected(n)
                    if 1 <= n <= CONV * BATCH:
                        first_tap(n - 1)
                    if 4 <= n < 4 + CONV * BATCH:
                        activate(n - 4)
                act.wait_ge(m_bc, 1)
                act.activation(grown[:].rearrange("p a t h -> p (a t h)"), bank[7][:, 0:2 * TILES * SHEADS], ACT.Exp).then_inc(m_E, 1)
                for i in range(TILES + 1):
                    r = i % 2
                    if i < TILES:
                        act.wait_ge(m_tp, i + 1)
                        past(act, m_s, i - 1)
                        act.activation(b_tok[:, r, :], bank[0][:, INNER:INNER + STATE], ACT.Copy).then_inc(m_B, 1)
                        act.wait_ge(m_df, i + 1)
                        past(act, m_xdd, i - 1)
                        past(act, m_M, i - 1)
                        act.activation(decay[:, r, :, :].rearrange("p h n -> p (h n)"), bank[2], ACT.Exp).then_inc(m_L, 1)
                    if i in (5, BT):
                        b = int(i == BT)
                        for u in range(CONV * BATCH + CONV * b, CONV * BATCH + CONV * (b + 1)):
                            activate(u)
                    if i < 4:
                        projected(early + 2 * i)
                        projected(early + 2 * i + 1)
                    if i < BATCH * CONV:
                        for u in range(0 if i == 0 else conv_by[i], conv_by[min(i + 1, BATCH * CONV - 1)]):
                            first_tap(CONV * BATCH + u)
                    if i >= 1:
                        act.wait_ge(m_yg, i)
                        past(act, m_o, i - 3)
                        act.activation(ysq[:, (i - 1) % 3, :, :], yg[:, (i - 1) % 3, :, :], ACT.Square).then_inc(m_sq, 1)

            if stage >= 1:
                experts(0, 1)
            if stage >= 2:
                state_space(2)
            if stage >= 3:
                experts(1, 3)
            act.wait_ge(s_x, 1)
            act.dma_start(out.rearrange("b (t p) d -> p (b t) d", p=P), x[:]).then_inc(s_out, 16)

        @block.tensor
        def _(pe):
            pe.wait_ge(s_w, 80)
            for i in range(3):
                pe.matmul(bank[4][:, i * P:(i + 1) * P], wqkv[:, i, :], ident[:], start=True, stop=True)
            pe.matmul(bank[4][:, 3 * P:4 * P], wqkv[:, 0, :], rot[:], start=True, stop=True).then_inc(s_wt, 1)
            pe.matmul(bank[5][:, 0:P], wqkv[:, 1, :], rot[:], start=True, stop=True).then_inc(s_wt, 1)

            def transpose_tiles(k, src, groups_of_tiles=range(4)):
                for i in groups_of_tiles:
                    pe.wait_ge(s_xn, 2 * k + i // 2 + 1)
                    past(pe, s_trc, 4 * k + i - 1)
                    for c in range(4):
                        ins = pe.transpose(tr_bank(k, i)[:, c * P:(c + 1) * P], src[:, 4 * i + c, 0:D], ident[:])
                    ins.then_inc(s_tr, 1)

            n = 0
            pe.wait_ge(s_wtc, 2)

            def values_of(i):
                past(pe, s_valc, i - 1)
                for k in range(4):
                    ins = pe.matmul(bank[4 + i % 2][:, k * P:(k + 1) * P], xnT[:, (4 * i + k) * P:(4 * i + k + 1) * P],
                                    wT[:, 2, :], start=True, stop=True)
                ins.then_inc(s_val, 1)

            for b in range(BATCH):
                transpose_tiles(0, xn, range(2 * b, 2 * b + 2))
                for side in range(2):
                    for h in range(2):
                        n += 1
                        pe.wait_ge(s_trc, 2 * b + h + 1)
                        past(pe, s_projc, n - 2)
                        rhs = xnT[:, b * SEQ + h * HALF:b * SEQ + (h + 1) * HALF]
                        pe.matmul(bank[(2 * n) % 4], wT[:, side, :], rhs, start=True, stop=True)
                        pe.matmul(bank[(2 * n + 1) % 4], wT[:, 3 + side, :], rhs, start=True, stop=True).then_inc(s_proj, 1)
                        if n >= 5:
                            values_of(n - 5)
            pe.wait_ge(s_valc, TILES // 4)
            pe.wait_ge(s_projc, 8)
            pe.wait_ge(s_init, 2)
            pe.wait_ge(s_id16, 1)

            def max_scores(n, slot, i, load_turn):
                if i == 0:
                    pe.wait_ge(s_load[slot], LOADS * 16 * (load_turn + 1))
                past(pe, s_mx, BT * n + i - 1)
                for h in range(2):
                    ins = pe.matmul(bank[2 * (i % 2) + h], qa[0:KROWS, slot, i * P:(i + 1) * P],
                                    ka[0:KROWS, slot, h * HALF:(h + 1) * HALF], start=True, stop=True)
                ins.then_inc(s_ms, 1)

            def max_transpose(n, outputs):
                pe.wait_ge(s_mp, n + 1)
                past(pe, s_oa, 2 * outputs)
                pe.transpose(mtrans, maxparts[:].rearrange("p a t -> p (a t)"), ident16[:]).then_inc(s_mt, 1)

            def scores(n, slot, i):
                if i == 0:
                    pe.wait_ge(s_mrow, 16 * PARTS * (n + 1))
                past(pe, s_pr, 16 * n + i - 1)
                pe.matmul(bank[4 + i % 2], ka[0:KROWS + PARTS, slot, (i // 2) * P:(i // 2 + 1) * P],
                          qa[0:KROWS + PARTS, slot, (i % 2) * HALF:(i % 2 + 1) * HALF], start=True, stop=True).then_inc(s_sc, 1)

            def values_product(n, vslot, k, p=0):
                if k == 0:
                    pe.wait_ge(s_vst, n + 1)
                    if vslot == 0:
                        past(pe, s_oc, p)
                pe.wait_ge(s_pr, 16 * n + 4 * k + 4)
                for e in range(2):
                    for h in range(2):
                        q = VCOL * (2 * e + h)
                        ins = pe.matmul(bank[6][q:q + VCOL, :], vstage[:, vslot, 2 * k + e, :],
                                        probs[:, (2 * k + e) % 4, h * HALF:(h + 1) * HALF],
                                        start=(k == 0 and vslot == 0), stop=(k == 3 and vslot == 1))
                ins.then_inc(s_pv, 1)

            def out_transpose(p, maxima_out):
                pe.wait_ge(s_oc, p + 1)
                past(pe, s_oa, 2 * p)
                pe.wait_ge(s_mc, maxima_out)
                for k in range(4):
                    ins = pe.transpose(bank[7][:, k * P:(k + 1) * P], o_sb[:, k * P:(k + 1) * P], ident[:])
                ins.then_inc(s_ot, 1)

            for i in range(BT):
                max_scores(0, 0, i, 0)
            max_transpose(0, 0)
            for i in range(BT):
                max_scores(1, 1, i, 0)

            def body(g, where):
                for j in range(4):
                    n = 4 * g + j
                    ahead = where < 2 or j < 2
                    turn = g + (j + 2) // 4
                    for k in range(4):
                        scores(n, j, 4 * k)
                        scores(n, j, 4 * k + 1)
                        if k > 0:
                            values_product(n, j % 2, k - 1, 2 * g + j // 2)
                        elif where > 0 or j > 0:
                            values_product(n - 1, (j + 1) % 2, 3)
                        scores(n, j, 4 * k + 2)
                        scores(n, j, 4 * k + 3)
                        if ahead:
                            max_scores(n + 2, (j + 2) % 4, 2 * k, turn)
                            max_scores(n + 2, (j + 2) % 4, 2 * k + 1, turn)
                        if k == 1 and (where < 2 or j < 3):
                            max_transpose(n + 1, 2 * g + (j - 1) // 2)
                        if k == 2 and j % 2 == 0 and (where > 0 or j > 0):
                            out_transpose(2 * g + j // 2 - 1, n + 2)

            pe.wait_ge(s_ones, 1)
            groups(pe, body)
            values_product(UNITS - 1, 1, 3)
            out_transpose(PAIRS - 1, UNITS)

            def experts(f, k):
                if f == 0:
                    pe.wait_ge(s_moew, 16 * 6)
                    pe.transpose(bank[5][:, 0:EXPERTS], router[:], ident[0:EXPERTS, 0:EXPERTS])
                    pe.transpose(bank[5][:, P:P + EXPERTS * FT], b1rows[:], ident[0:EXPERTS * FT, 0:EXPERTS * FT]).then_inc(s_wt, 1)
                transpose_tiles(k, xn)
                pe.wait_ge(s_wtc, 3)
                for q in range(4):
                    pe.wait_ge(s_trc, 4 * k + q + 1)
                    ins = pe.matmul(bank[4][q * QUAD:(q + 1) * QUAD, :], routerT[:], xnT[:, q * HALF:(q + 1) * HALF],
                                    start=True, stop=True)
                ins.then_inc(s_lt, 1)
                pe.wait_ge(s_lc, f + 1)
                for c in range(4):
                    ins = pe.transpose(bank[4][:, c * P:(c + 1) * P], prow[:, c * P:(c + 1) * P], ident[:])
                ins.then_inc(s_rt, 1)
                pe.wait_ge(s_ew, 32 * EXPERTS)


                def dense_hidden(i):
                    h = hs(f, 0, i)
                    if i >= 2:
                        pe.wait_ge(s_ha, acts(f) + i - 1)
                    pe.matmul(bank[(5, 7)[i % 2]], w1[:, 0, (i % FT) * P:(i % FT + 1) * P],
                              xnT[:, (i // FT) * HALF:(i // FT + 1) * HALF], start=True, stop=True).then_inc(s_h, 1)

                def dense_out(i):
                    g = i // 4
                    pe.wait_ge(s_ha, acts(f) + 4 * g + 4)
                    if i % 4 == 0:
                        past(pe, s_yc, ys(f, g))
                    for c in range(FT):
                        ins = pe.matmul(bank[6][:, (i % 4) * D:(i % 4 + 1) * D],
                                        hidden[:, g % 2, c, (i % 4) * P:(i % 4 + 1) * P], w2[:, 0, c, :],
                                        start=(c == 0), stop=(c == FT - 1))
                    if i % 4 == 3:
                        ins.then_inc(s_y, 1)

                dense = ([(dense_hidden, i) for i in range(2 * FT)] + [(dense_out, i) for i in range(4)] +
                         [(dense_hidden, i) for i in range(2 * FT, 3 * FT)] + [(dense_out, i) for i in range(4, 8)] +
                         [(dense_hidden, i) for i in range(3 * FT, 4 * FT)] + [(dense_out, i) for i in range(8, 16)])
                for step, i in dense[:EARLY]:
                    step(i)
                for c in range(4):
                    pe.wait_ge(s_dg, 4 * f + c + 1)
                    pe.matmul(bank[c], ones[:], diag[:, 4 * c:4 * c + 4, :].rearrange("p t n -> p (t n)"),
                              start=True, stop=True).then_inc(s_pw, 1)
                pe.wait_ge(s_oh, f + 1)
                for n in range(STEPS):
                    g, j = n // TILES, n % TILES
                    if j == 0:
                        pe.wait_ge(s_pwc, 4 * f + g + 1)
                    pe.wait_ge(s_bf, STEPS * f + n + 1)
                    for i in range(4):
                        ins = pe.matmul(bank[g][:, i * EXPERTS:(i + 1) * EXPERTS], before[:, n % RANK_RING, i * P:(i + 1) * P],
                                        onehot[:, j, :], start=(j == 0 and i == 0), stop=(j == TILES - 1),
                                        skip_group_check=True)
                    ins.then_inc(s_rk, 1)
                    if n % 3 == 2:
                        step, i = dense[EARLY + n // 3]
                        step(i)
                for step, i in dense[EARLY + STEPS // 3:]:
                    step(i)

                def sorted_in(e):
                    pe.wait_ge(s_srt[e], 32 * (f + 1))
                    if e == 1:
                        pe.wait_ge(s_ha, acts(f) + 16)
                    elif e > 2:
                        pe.wait_ge(s_stc, (EXPERTS - 1) * f + e - 2)
                    for m in range(CT):
                        n = min(P, CAP - m * P)
                        ins = pe.transpose(bank[(4, 7)[e % 2]][:, m * P:m * P + n], sorted_x[0:n, e, m, 0:D], ident[0:n, 0:n])
                    ins.then_inc(s_st, 1)

                def sparse_hidden(e):
                    pe.wait_ge(s_stc, (EXPERTS - 1) * f + e)
                    if e == 1:
                        pe.wait_ge(s_slot, 4 * f + 4)
                    for i in range(FT):
                        if e > 1:
                            if i % 2 == 0:
                                pe.wait_ge(s_ha, acts(f) + 16 + 2 * (e - 2) + i // 2 + 1)
                            else:
                                pe.wait_ge(s_hv, 2 * (EXPERTS - 1) * f + 2 * (e - 2) + i // 2 + 1)
                        pe.matmul(bank[i][:, 0:CAP], w1[:, e, i * P:(i + 1) * P], sortedT[:, (e - 1) * CAP:e * CAP],
                                  start=True, stop=True).then_inc(s_h, 1)

                def sparse_out(e):
                    pe.wait_ge(s_ha, acts(f) + 16 + 2 * e)
                    pe.wait_ge(s_hv, 2 * (EXPERTS - 1) * f + 2 * e)
                    pe.wait_ge(s_yc, ys(f, 3 + e - 2) + 1 if e > 1 else ys(f, 3) + 1)
                    for m in range(CT):
                        n = min(P, CAP - m * P)
                        for c in range(FT):
                            ins = pe.matmul(bank[5 + e % 2][0:n, m * D:(m + 1) * D], hidden[:, e % 2, c, m * P:m * P + n],
                                            w2[:, e, c, :], start=(c == 0), stop=(c == FT - 1))
                    ins.then_inc(s_y, 1)

                sorted_in(1)
                sorted_in(2)
                sparse_hidden(1)
                for e in range(1, EXPERTS):
                    if e < EXPERTS - 1:
                        sparse_hidden(e + 1)
                    if e < EXPERTS - 2:
                        sorted_in(e + 2)
                    sparse_out(e)

            def state_space(kt):
                pe.wait_ge(m_w, 16 * 15)
                for c in range(6):
                    ins = pe.transpose(bank[c // 4][:, (c % 4) * P:(c % 4 + 1) * P], win_rows[:, c, :], ident[:])
                    if c == 3:
                        ins.then_inc(m_wt, 1)
                pe.transpose(bank[1][:, 2 * P:2 * P + SHEADS], wdt_rows[:], ident[0:SHEADS, 0:SHEADS]).then_inc(m_wt, 1)
                for c in range(XC):
                    ins = pe.transpose(bank[2][:, c * P:(c + 1) * P], wout_rows[:, c * P:(c + 1) * P], ident[:])
                ins.then_inc(m_wt, 1)
                transpose_tiles(kt, un)
                pe.wait_ge(m_wc, 5)
                for q in range(4):
                    pe.wait_ge(s_trc, 4 * kt + q + 1)
                    ins = pe.matmul(bank[4][q * QUAD:(q + 1) * QUAD, :], wdtT[:], xnT[:, q * HALF:(q + 1) * HALF],
                                    start=True, stop=True)
                ins.then_inc(m_lt, 1)

                def project(n):
                    h, b, j = projections[n]
                    c = XC + j if j < CONV else j - CONV
                    past(pe, m_zc, n - 3 if n < early else n)
                    pe.matmul(bank[n % 4] if n < early else bank[3], winT[:, c * P:(c + 1) * P],
                              xnT[:, b * SEQ + h * HALF:b * SEQ + (h + 1) * HALF], start=True, stop=True).then_inc(m_zx, 1)

                for n in range(2):
                    project(n)
                pe.wait_ge(m_lc, 1)
                for c in range(4):
                    ins = pe.transpose(bank[4][:, c * P:(c + 1) * P], dtT[:, c * P:(c + 1) * P], ident[:])
                ins.then_inc(m_dt, 1)
                for n in range(2, early):
                    project(n)
                pe.wait_ge(m_dec, 1)
                decays = log_decay[:].rearrange("p t h -> p (t h)")
                pe.matmul(bank[7][:, 0:TILES * SHEADS], upto[:], decays, start=True, stop=True)
                pe.matmul(bank[7][:, TILES * SHEADS:2 * TILES * SHEADS], ones[:], decays, start=True, stop=True).then_inc(m_bc, 1)
                pe.wait_ge(m_zc, early)

                def chunk_a(i):
                    T, b, c = chunk_tile(i), i % 2, i // 2
                    cols = slice(T * P, (T + 1) * P)
                    past(pe, m_xd, i)
                    past(pe, m_B, i)
                    pe.wait_ge(m_xbc, CONV * (b + 1) if c < BT // 2 else CONV * (BATCH + b + 1))
                    for ct in range(XC + 1):
                        ins = pe.transpose(bank[0][:, ct * P:(ct + 1) * P], xbc[:, ct, cols], ident[:])
                    ins.then_inc(m_tp, 1)
                    pe.wait_ge(m_ua, i + 1)
                    past(pe, m_L, i)
                    for h in range(SHEADS):
                        ins = pe.matmul(bank[2][:, h * P:(h + 1) * P], seg[:, i % 2, h, :], upto[:], start=True, stop=True)
                    ins.then_inc(m_df, 1)
                    past(pe, m_gm, i)
                    past(pe, m_yb, i - 2)
                    pe.matmul(bank[1][:, 0:P], xbc[:, XC, cols], xbc[:, XC + 1, cols], start=True, stop=True).then_inc(m_g, 1)

                def before_chunk(i):
                    T, b, c = chunk_tile(i), i % 2, i // 2
                    cols = slice(T * P, (T + 1) * P)
                    if c > 0:
                        pe.wait_ge(m_gm, i + 1)
                        pe.wait_ge(m_st, i - 1)
                        pe.matmul(bank[1][:, P:P + INNER], xbc[:, XC + 1, cols],
                                  state[:, b, c % 2, :, :].rearrange("p h w -> p (h w)"), start=True, stop=True).then_inc(m_yo, 1)

                def chunk_b(i):
                    r, b, c = i % 2, i % 2, i // 2
                    pe.wait_ge(m_M, i + 1)
                    pe.wait_ge(m_xd, i + 1)
                    past(pe, m_u, i)
                    for h in range(SHEADS):
                        dst = bank[4][(h % 2) * SW:(h % 2 + 1) * SW, (h // 2) * P:(h // 2 + 1) * P]
                        ins = pe.matmul(dst, xd[:, r, h, :], mix[:, r, h, :], start=(h < 2), stop=(c == 0), skip_group_check=True)
                    if c > 0:
                        pe.wait_ge(m_yb, i - 1)
                        for ct in range(XC):
                            ins = pe.matmul(bank[4][:, ct * P:(ct + 1) * P], y_before[:, r, 2 * ct:2 * ct + 2, :].rearrange("p h w -> p (h w)"),
                                            ident[:], start=False, stop=True, skip_group_check=True)
                    ins.then_inc(m_y, 1)
                    pe.wait_ge(m_B, i + 1)
                    pe.wait_ge(m_xdd, i + 1)
                    past(pe, m_st, i)
                    pe.matmul(bank[5][:, 0:INNER], b_tok[:, r, :], xdd[:, r, :, :].rearrange("p h w -> p (h w)"),
                              start=True, stop=True).then_inc(m_s, 1)

                def chunk_c(i):
                    r = i % 2
                    pe.wait_ge(m_sq, i + 1)
                    past(pe, m_fin, i - 1)
                    for c in range(XC):
                        pe.matmul(bank[6 + r][:, P:2 * P], ysq[:, i % 3, c, :], ones[:], start=(c == 0), stop=(c == XC - 1))
                    for c in range(XC):
                        ins = pe.matmul(bank[6 + r][:, 0:P], yg[:, i % 3, c, :], woutT[:, c, :], start=(c == 0), stop=(c == XC - 1))
                    ins.then_inc(m_o, 1)

                for i in range(TILES + 3):
                    if i < TILES:
                        chunk_a(i)
                    if i < 4:
                        project(early + 2 * i)
                    if 1 <= i <= TILES:
                        chunk_b(i - 1)
                    if i < 4:
                        project(early + 2 * i + 1)
                    if i < TILES:
                        before_chunk(i)
                    if i >= 3:
                        chunk_c(i - 3)

            if stage >= 1:
                experts(0, 1)
            if stage >= 2:
                state_space(2)
            if stage >= 3:
                experts(1, 3)


def shape_constants():
    import numpy as np
    c = {}
    c["ident"] = np.eye(P, dtype=np.float32)
    rot = np.zeros((P, P), np.float32)
    for i in range(0, P, 2):
        rot[i + 1, i] = -1.0
        rot[i, i + 1] = 1.0
    c["rot"] = rot
    row, col = np.arange(P)[:, None], np.arange(P)[None, :]
    c["after"] = (row > col).astype(np.float32)
    c["upto"] = (row <= col).astype(np.float32)
    c["left"] = np.tile(EXPERTS - np.arange(EXPERTS, dtype=np.float32), (P, 1))
    c["own_row"] = (SLOTS + np.arange(TOK, dtype=np.float32)).reshape(TILES, P).T.copy()
    c["tri_tiny"] = np.where(np.arange(P)[:, None] < np.arange(7 * P)[None, :] - 3 * P, np.float32(TINY), np.float32(0)).astype(np.float32)
    c["spare_row"] = (TOK + np.arange(SLOTS, dtype=np.float32)).reshape(SLOTS, 1)
    inv = (np.float32(1.0) / np.float32(10000.0) ** (np.arange(0, HD, 2, dtype=np.float32) / np.float32(HD))).astype(np.float32)
    ang = np.outer(np.arange(SEQ, dtype=np.float32), inv).astype(np.float32)
    rows = (np.arange(P) % HD) // 2
    c["cos"] = np.ascontiguousarray(np.cos(ang).astype(np.float32).T[rows])
    c["sin"] = np.ascontiguousarray(np.sin(ang).astype(np.float32).T[rows])
    return c


_INS = ['L0_attn_a_x', 'L0_attn_a_wq', 'L0_attn_a_wk', 'L0_attn_a_wv', 'L0_attn_b_norm_w', 'L0_attn_b_in_proj_w',
        'L0_attn_b_conv_w', 'L0_attn_b_conv_b', 'L0_attn_b_dt_bias', 'L0_attn_b_A_log', 'L0_attn_b_D',
        'L0_attn_b_gnorm_w', 'L0_attn_b_out_proj_w', 'L0_ffn_router_w', 'L0_ffn_W1', 'L0_ffn_b1', 'L0_ffn_W2',
        'L0_ffn_b2']


def kernel(**inputs):
    import numpy as _np
    import concourse.bacc as _bacc
    from concourse import mybir as _mybir
    from concourse.bass_utils import run_bass_kernel_spmd as _run

    nc = _bacc.Bacc("TRN2", target_bir_lowering=False, num_devices=1)
    arrays, tensors = {}, {}
    for name, a in [(n, inputs[n]) for n in _INS] + list(shape_constants().items()):
        a = _np.ascontiguousarray(a)
        arrays[f"in_{name}_dram"] = a
        tensors[name] = nc.dram_tensor(f"in_{name}_dram", a.shape, _mybir.dt.from_np(a.dtype), kind="ExternalInput").ap()
    out = nc.dram_tensor("out_0_dram", (BATCH, SEQ, D), _mybir.dt.float32, kind="ExternalOutput").ap()
    bass_hybrid(nc, tensors, out)
    r = _run(nc, [arrays], core_ids=[0])
    return r.results[0]["out_0_dram"]
```
